# Optimizing a Trainium2 kernel written in Bass

```python
import numpy as np
import jax
import jax.numpy as jnp

def _softmax(x, axis=-1):
    return jax.nn.softmax(x, axis=axis)

def _gelu(x):
    return jax.nn.gelu(x, approximate=True)

def _silu(x):
    return jax.nn.silu(x)

def _sigmoid(x):
    return jax.nn.sigmoid(x)

def _layernorm(x, axis=-1, eps=1e-05):
    m = jnp.mean(x, axis=axis, keepdims=True)
    v = jnp.var(x, axis=axis, keepdims=True)
    return (x - m) / jnp.sqrt(v + eps)

def _scatter_add(tgt, idx, src, axis=0):
    return tgt.at[idx].add(src)

def _segment_sum(src, seg, n):
    return jax.ops.segment_sum(src, seg, n)
kernel_name = 'mk_perceiver_d1_seqx_r4_b5f116'

def setup_inputs(seed: int=0):
    np.random.seed(seed)
    _w = jnp.asarray

    def _rec_inputs():
        import jax
        import jax.numpy as jnp
        _rk = jax.random.key(seed)
        x = 7.22e-05 + 1 * jax.random.normal(jax.random.fold_in(_rk, 1), (2, 256, 256), jnp.float32)
        _lenS = 256 - jax.random.randint(jax.random.fold_in(_rk, 7), (2,), 0, max(1, 256 // 4) + 1, jnp.int32)
        _lenS2 = 4096 - jax.random.randint(jax.random.fold_in(_rk, 8), (2,), 0, max(1, 4096 // 4) + 1, jnp.int32)
        _ctx_1024P = jax.random.normal(jax.random.fold_in(_rk, 11), (2, 16, 256), jnp.float32)
        _ctx_1024c = jax.random.dirichlet(jax.random.fold_in(_rk, 511), 0.3 * jnp.ones((16,), jnp.float32), (2, 4096))
        _ctx_1024t = jnp.einsum('bsk,bkd->bsd', _ctx_1024c, _ctx_1024P)
        _ctx_1024t = _ctx_1024t * jax.lax.rsqrt(jnp.mean(jnp.square(_ctx_1024t)) + 1e-12) * 0.953939
        ctx_1024 = 4.13588e-05 + 0.999923 * (_ctx_1024t + 0.3 * jax.random.normal(jax.random.fold_in(_rk, 611), (2, 4096, 256), jnp.float32))
        _validS = jnp.arange(256)[None, :] < _lenS[:, None]
        _validS2 = jnp.arange(4096)[None, :] < _lenS2[:, None]
        _causal = jnp.tril(jnp.ones((256, 256), dtype=bool))
        mask_1x1xSxS2_bk0 = jnp.logical_not(jnp.broadcast_to(_validS2[0:1, None, None, :], (1, 1, 256, 4096)))
        return (x, ctx_1024, mask_1x1xSxS2_bk0)
    x, ctx_1024, mask_1x1xSxS2_bk0 = _rec_inputs()

    def _L0_xattn_setup():
        import jax, jax.numpy as jnp
        import numpy as np
        N, L, E, H = (4, 512, 256, 16)
        D = E // H
        SCALE = D ** 0.5

        def _proj(x, w):
            n, l, _ = x.shape
            return (x @ w.T).reshape(n, l, H, D).transpose(0, 2, 1, 3)
        key = jax.random.key(seed)
        ks = jax.random.split(key, 7)
        inp = {'query': jax.random.normal(ks[0], (N, L, E), dtype=jnp.float32), 'key': jax.random.normal(ks[1], (N, L, E), dtype=jnp.float32), 'value': jax.random.normal(ks[2], (N, L, E), dtype=jnp.float32), 'wq': jax.random.normal(ks[3], (E, E), dtype=jnp.float32) * E ** (-0.5), 'wk': jax.random.normal(ks[4], (E, E), dtype=jnp.float32) * E ** (-0.5), 'wv': jax.random.normal(ks[5], (E, E), dtype=jnp.float32) * E ** (-0.5), 'wo': jax.random.normal(ks[6], (E, E), dtype=jnp.float32) * E ** (-0.5), 'mask': jnp.tril(jnp.ones((L, L), dtype=bool))[None, None, :, :]}
        return inp
    _L0_xattn_all = _L0_xattn_setup()
    _L0_xattn_in = {k: v for k, v in _L0_xattn_all.items() if k in ('wq', 'wk', 'wv', 'wo')}
    del _L0_xattn_all

    def _L0_attn_setup():
        import jax, jax.numpy as jnp
        import numpy as np
        HIDDEN = 256
        HEADS = 16
        key = jax.random.key(seed)
        ks = jax.random.split(key, 7)
        s = 1.0 / np.sqrt(HIDDEN)
        return {'x': jax.random.normal(ks[0], (4, 1024, HIDDEN), dtype=jnp.float32), 'Wq': jax.random.uniform(ks[1], (HIDDEN, HIDDEN), jnp.float32, -s, s), 'bq': jax.random.uniform(ks[2], (HIDDEN,), jnp.float32, -s, s), 'Wk': jax.random.uniform(ks[3], (HIDDEN, HIDDEN), jnp.float32, -s, s), 'bk': jax.random.uniform(ks[4], (HIDDEN,), jnp.float32, -s, s), 'Wv': jax.random.uniform(ks[5], (HIDDEN, HIDDEN), jnp.float32, -s, s), 'bv': jax.random.uniform(ks[6], (HIDDEN,), jnp.float32, -s, s)}
    _L0_attn_all = _L0_attn_setup()
    _L0_attn_in = {k: v for k, v in _L0_attn_all.items() if k in ('Wq', 'bq', 'Wk', 'bk', 'Wv', 'bv')}
    del _L0_attn_all

    def _L0_ffn_setup():
        import jax, jax.numpy as jnp
        import numpy as np
        FF_DIM = 512
        TOP_K = 2
        key = jax.random.key(seed)
        k1, k2, k3, k4 = jax.random.split(key, 4)
        B, S, D, E, F = (2, 512, 256, 8, FF_DIM)
        std = 0.006
        return {'x': jax.random.normal(k1, (B, S, D), dtype=jnp.float32), 'gate_w': jax.random.normal(k2, (D, E), dtype=jnp.float32) * 0.02, 'gate_up_w': jax.random.normal(k3, (E, D, 2 * F), dtype=jnp.float32) * std, 'down_w': jax.random.normal(k4, (E, F, D), dtype=jnp.float32) * std}
    _L0_ffn_all = _L0_ffn_setup()
    _L0_ffn_in = {k: v for k, v in _L0_ffn_all.items() if k in ('gate_w', 'gate_up_w', 'down_w')}
    del _L0_ffn_all
    return {'x': x, 'ctx_1024': ctx_1024, 'mask_1x1xSxS2_bk0': mask_1x1xSxS2_bk0, 'L0_xattn_wq': _L0_xattn_in['wq'], 'L0_xattn_wk': _L0_xattn_in['wk'], 'L0_xattn_wv': _L0_xattn_in['wv'], 'L0_xattn_wo': _L0_xattn_in['wo'], 'L0_attn_Wq': _L0_attn_in['Wq'], 'L0_attn_bq': _L0_attn_in['bq'], 'L0_attn_Wk': _L0_attn_in['Wk'], 'L0_attn_bk': _L0_attn_in['bk'], 'L0_attn_Wv': _L0_attn_in['Wv'], 'L0_attn_bv': _L0_attn_in['bv'], 'L0_ffn_gate_w': _L0_ffn_in['gate_w'], 'L0_ffn_gate_up_w': _L0_ffn_in['gate_up_w'], 'L0_ffn_down_w': _L0_ffn_in['down_w']}

def reference(x, ctx_1024, mask_1x1xSxS2_bk0, L0_xattn_wq, L0_xattn_wk, L0_xattn_wv, L0_xattn_wo, L0_attn_Wq, L0_attn_bq, L0_attn_Wk, L0_attn_bk, L0_attn_Wv, L0_attn_bv, L0_ffn_gate_w, L0_ffn_gate_up_w, L0_ffn_down_w):
    import jax
    import jax.numpy as jnp

    def _L0_xattn_ref(query, key, value, wq, wk, wv, wo, mask):
        import jax, jax.numpy as jnp
        import numpy as np
        N, L, E, H = (4, 512, 256, 16)
        D = E // H
        SCALE = D ** 0.5

        def _proj(x, w):
            n, l, _ = x.shape
            return (x @ w.T).reshape(n, l, H, D).transpose(0, 2, 1, 3)
        q = _proj(query, wq)
        k = _proj(key, wk)
        v = _proj(value, wv)
        scores = jnp.einsum('nhqd,nhkd->nhqk', q, k) / SCALE
        scores = jnp.where(mask, scores, -jnp.inf)
        attn = jax.nn.softmax(scores, axis=-1)
        out = jnp.einsum('nhqk,nhkd->nhqd', attn, v)
        out = out.transpose(0, 2, 1, 3).reshape(query.shape[0], query.shape[1], H * D)
        return out @ wo.T

    def _L0_attn_ref(x, Wq, bq, Wk, bk, Wv, bv):
        import jax, jax.numpy as jnp
        import numpy as np
        HIDDEN = 256
        HEADS = 16
        batch, len_, hidden = x.shape
        xh = x.reshape(batch, HEADS, len_ // HEADS, hidden)
        q = jnp.einsum('bhcd,ed->bhce', xh, Wq) + bq
        k = jnp.einsum('bhcd,ed->bhce', xh, Wk) + bk
        v = jnp.einsum('bhcd,ed->bhce', xh, Wv) + bv
        score = jax.nn.softmax(jnp.einsum('bhce,bhke->bhck', q, k), axis=-1)
        out = jnp.einsum('bhck,bhke->bhce', score, v)
        return out.reshape(batch, len_, hidden)

    def _L0_ffn_ref(x, gate_w, gate_up_w, down_w):
        import jax, jax.numpy as jnp
        import numpy as np
        FF_DIM = 512
        TOP_K = 2
        B, S, D = x.shape
        E = gate_up_w.shape[0]
        F = down_w.shape[1]
        x_flat = x.reshape(B * S, D)
        router_logits = x_flat @ gate_w
        router_probs = jax.nn.softmax(router_logits, axis=-1)
        top_k_probs, top_k_idx = jax.lax.top_k(router_probs, TOP_K)
        top_k_probs = top_k_probs / jnp.sum(top_k_probs, axis=-1, keepdims=True)
        gate_up = jnp.einsum('nd,edh->enh', x_flat, gate_up_w)
        gate_out = gate_up[..., :F]
        up_out = gate_up[..., F:]
        hidden = jax.nn.silu(gate_out) * up_out
        expert_out = jnp.einsum('enf,efd->end', hidden, down_w)
        out_t = jnp.transpose(expert_out, (1, 0, 2))
        sel = jnp.take_along_axis(out_t, top_k_idx[:, :, None], axis=1)
        output = jnp.sum(sel * top_k_probs[:, :, None], axis=1)
        return output.reshape(B, S, D)
    x = x + _L0_xattn_ref(_layernorm(x, axis=-1), ctx_1024, ctx_1024, L0_xattn_wq, L0_xattn_wk, L0_xattn_wv, L0_xattn_wo, mask_1x1xSxS2_bk0)
    x = x + _L0_attn_ref(_layernorm(x, axis=-1), L0_attn_Wq, L0_attn_bq, L0_attn_Wk, L0_attn_bk, L0_attn_Wv, L0_attn_bv)
    x = x + _L0_ffn_ref(_layernorm(x, axis=-1), L0_ffn_gate_w, L0_ffn_gate_up_w, L0_ffn_down_w)
    return x

_drawn_inputs = setup_inputs


def setup_inputs(seed=0):
    import zlib

    import numpy as np

    out = dict(_drawn_inputs(seed))
    spreads = {}
    factors = {'L0_attn_bk': 8.0, 'L0_ffn_gate_w': 8.0, 'L0_ffn_gate_up_w': 8.0, 'L0_ffn_down_w': 8.0}
    for name, (base, spread) in spreads.items():
        noise = np.random.default_rng([zlib.crc32(name.encode()), seed]).standard_normal(out[name].shape)
        drawn = base * np.exp(spread * noise) if base else spread * noise
        out[name] = jnp.asarray(drawn.astype(out[name].dtype))
    for name, factor in factors.items():
        out[name] = (out[name] * factor).astype(out[name].dtype)
    return out
```

```python
from contextlib import ExitStack

import concourse.bass as bass
from concourse import mybir

F32 = mybir.dt.float32
BF16 = mybir.dt.bfloat16
I32 = mybir.dt.int32
U8 = mybir.dt.uint8
ALU = mybir.AluOpType
ACT = mybir.ActivationFunctionType
AX = mybir.AxisListType.X

P = 128
B, Q, E, S = 2, 256, 256, 4096
H, D = 16, 16
NH = B * H
T = B * Q // P
KIN = E // P
CK = 512
NC = S // CK
KT = S // P
UNITS = 8
UK = S // UNITS
UT = UK // P
STEPS = NH * UNITS
GROUP = 16
NE, F = 8, 512
FT = F // P
PARTS = 3
STACK = 6 * D
ROWS = STACK + PARTS
LEAD_A = 14
LEAD_B = 3
PE_UNITS = (1, 4, 6)
POOL_UNITS = tuple(u for u in range(UNITS) if u not in PE_UNITS)
BIG = 3.0e38
EPS = 1e-5
SLOTS = 4
LOADS = 6


def perceiver_block(nc, x, ctx_in, mask_q, mask_k, wq, wk, wv, wo, sq, bq, sk, bk, sv, bv, gate_w, up_w, down_w, out):
    k_parts = nc.dram_tensor("k_parts", (PARTS, NH, D, S), BF16, kind="Internal").ap()
    q_parts = nc.dram_tensor("q_parts", (PARTS, NH, D, Q), BF16, kind="Internal").ap()

    with ExitStack() as ctx:
        def sb(name, shape, dt=F32):
            return ctx.enter_context(nc.sbuf_tensor(name, shape, dt))

        def sem(name):
            return ctx.enter_context(nc.semaphore(name))

        V = sb("V", [P, NH, KT, D])
        kst = sb("kst", [P, SLOTS, S], BF16)
        qst = sb("qst", [P, SLOTS, Q], BF16)
        mask_bias = sb("mask_bias", [P, Q // P, S], BF16)
        mask_turned = sb("mask_turned", [P, len(PE_UNITS), UT, Q], BF16)
        mask_int = sb("mask_int", [P, len(POOL_UNITS), UT, Q], I32)
        probs = sb("probs", [P, 4, UT * Q])
        Vh = sb("Vh", [P, 2, KT, 32])
        unused = sb("unused", [P, 2, UK], BF16)
        xs = sb("xs", [P, T, E])
        xn = sb("xn", [P, T, E])
        xnT = sb("xnT", [P, KIN, B * Q])
        w_q = sb("w_q", [P, KIN, E])
        w_k = sb("w_k", [P, KIN, E])
        w_v = sb("w_v", [P, KIN, E])
        w_o = sb("w_o", [P, KIN, E])
        rest = sb("rest", [P, 2, CK])
        unit_max = sb("unit_max", [P, 2, Q // P, UNITS])
        head_max = sb("head_max", [P, 2, Q // P])
        neg_parts = sb("neg_parts", [P, 2, Q // P, 4], BF16)
        neg_rest = sb("neg_rest", [P, 2, Q // P])
        any_kept = sb("any_kept", [P, NH, Q // P])
        oT = sb("oT", [P, 2, Q])
        O = sb("O", [P, NH, Q // P, D + 1])
        norm = sb("norm", [P, NH, Q // P])
        ident = sb("ident", [P, P])
        ident_bf = sb("ident_bf", [P, P], BF16)
        fold = sb("fold", [P, 32])
        stats = sb("stats", [P, T, 6])
        mean_var = sb("mean_var", [P, T, 2])
        var_eps = sb("var_eps", [P, T])
        rstd = sb("rstd", [P, T])
        neg_half = sb("neg_half", [P, T])
        bias_qk = sb("bias_qk", [P, 2, KIN])
        bias_v = sb("bias_v", [1, E])
        ones_row = sb("ones_row", [1, P])
        group_bias = sb("group_bias", [P, P // GROUP, GROUP])
        w_g = sb("w_g", [P, KIN, NE])
        rank = sb("rank", [P, NE])
        lg = sb("lg", [P, 8, T, NE])
        tk = sb("tk", [P, 8, T])
        wgt = sb("wgt", [P, NE, T])

        ctx_buf = kst[:, 2, :].bitcast(F32).rearrange("p (j a k) -> p j a k", j=2, a=KIN)
        kp = kst[:, 3, 0:2 * PARTS * CK].rearrange("p (j a k) -> p j a k", j=2, a=PARTS)
        V_flat = V[:].rearrange("p h k d -> p (h k d)")
        half = H * KT * D
        qp = V_flat[:, half:2 * half].bitcast(BF16)[:, 0:PARTS * KIN * B * Q].rearrange(
            "p (a e t) -> p a e t", a=PARTS, e=KIN)
        raw = probs[:].rearrange("p a k -> p (a k)").bitcast(U8)
        raw_q = raw[:, 0:(Q // P) * S].rearrange("p (t k) -> p t k", t=Q // P)
        raw_k = raw[:, (Q // P) * S:(Q // P) * S + KT * Q].rearrange("p (k q) -> p k q", k=KT)
        up_sb = V_flat[:, 0:2 * KIN * 2 * F].rearrange("p (s a n) -> p s a n", s=2, a=KIN)
        down_sb = V_flat[:, 4096:4096 + 2 * FT * E].rearrange("p (s a n) -> p s a n", s=2, a=FT)
        at = half
        q2T = V_flat[:, at:at + 1024].rearrange("p (a t) -> p a t", a=KIN)
        k2T = V_flat[:, at + 1024:at + 2048].rearrange("p (a t) -> p a t", a=KIN)
        v2 = V_flat[:, at + 2048:at + 3072].rearrange("p (t e) -> p t e", t=T)
        hid = V_flat[:, at + 4096:at + 8192].rearrange("p (s f t) -> p s f t", s=2, f=FT)
        free2 = mask_bias[:].rearrange("p t k -> p (t k)").bitcast(F32)
        attn = free2[:, 0:1024].rearrange("p (t e) -> p t e", t=T)
        aT = free2[:, 1024:2048].rearrange("p (t e) -> p t e", t=T)
        s2 = free2[:, 2048:2560].rearrange("p (t k) -> p t k", t=T)
        p2 = free2[:, 2560:3072].rearrange("p (t k) -> p t k", t=T)
        p2T = free2[:, 3072:3584].rearrange("p (t k) -> p t k", t=T)
        silu = free2[:, 3584 - 512:4096].rearrange("p (s t) -> p s t", s=2)

        ps_a = ctx.enter_context(nc.psum_tensor("ps_a", [P, 2, 512], F32))
        ps_b = ctx.enter_context(nc.psum_tensor("ps_b", [P, 2, 1024], F32))
        ps_v = ctx.enter_context(nc.psum_tensor("ps_v", [P, 512], F32))
        ps_m = ctx.enter_context(nc.psum_tensor("ps_m", [P, 512], F32))
        BANK = [ps_a[:, 0, :], ps_a[:, 1, :], ps_b[:, 0, 0:512], ps_b[:, 0, 512:1024],
                ps_b[:, 1, 0:512], ps_b[:, 1, 512:1024], ps_v[:, :], ps_m[:, :]]
        max_rows = ps_m[STACK:STACK + PARTS, 0:Q]
        o_cols = ps_m[:, Q:Q + 64].rearrange("p (t d) -> p t d", t=2)

        x_in, wq_in, wk_in, wv_in, wo_in, small_in = (sem(n) for n in ("x_in", "wq_in", "wk_in", "wv_in", "wo_in", "small_in"))
        mask_in, self_in, out_done = sem("mask_in"), sem("self_in"), sem("out_done")
        ctx_in_s = [sem(f"ctx_in{j}") for j in range(2)]
        k_out = [[sem(f"k_out{b}{e}") for e in range(2)] for b in range(B)]
        q_out = sem("q_out")
        stack_in = [sem(f"stack_in{j}") for j in range(SLOTS)]
        up_in = [sem(f"up_in{j}") for j in range(2)]
        down_in = [sem(f"down_in{j}") for j in range(2)]
        pool_consts, dve_consts, consts, ones_set, dve_own = (sem(n) for n in ("pool_consts", "dve_consts", "consts", "ones_set", "dve_own"))
        var_ready, rstd_ready, xn_ready, xnT_ps, xnT_ready = (sem(n) for n in ("var_ready", "rstd_ready", "xn_ready", "xnT_ps", "xnT_ready"))
        masks_ready = sem("masks_ready")
        k_ps, kh_ready, km_ready, v_ps = (sem(n) for n in ("k_ps", "kh_ready", "km_ready", "v_ps"))
        k_rest = [sem(f"k_rest{j}") for j in range(2)]
        kl_ready = [sem(f"kl_ready{e}") for e in range(2)]
        v_stored = [sem(f"v_stored{j}") for j in range(2)]
        q_ps, q_high, q_split = sem("q_ps"), sem("q_high"), sem("q_split")
        a_ps, tiles_seen, a_max, chain, neg_ready, rows_ps, rows_ready = (sem(n) for n in ("a_ps", "tiles_seen", "a_max", "chain", "neg_ready", "rows_ps", "rows_ready"))
        b_ps, exp_done, pool_masked, pv_done, vh_ready = (sem(n) for n in ("b_ps", "exp_done", "pool_masked", "pv_done", "vh_ready"))
        oT_ready, o_ps, o_stored = sem("oT_ready"), sem("o_ps"), sem("o_stored")
        attn_ready, aT_ps, aT_ready, wo_ps = (sem(n) for n in ("attn_ready", "aT_ps", "aT_ready", "wo_ps"))
        qk2_ps, qk2_ready, v2_ps, v2_ready = (sem(n) for n in ("qk2_ps", "qk2_ready", "v2_ps", "v2_ready"))
        s2_ps, s2_ready, p2_ready, p2T_ps, p2T_ready, o2_ps = (sem(n) for n in ("s2_ps", "s2_ready", "p2_ready", "p2T_ps", "p2T_ready", "o2_ps"))
        gate_ps, gate_sub, gate_exp = sem("gate_ps"), sem("gate_sub"), sem("gate_exp")
        up_ps, silu_ready, hid_ready, down_ps, summed = (sem(n) for n in ("up_ps", "silu_ready", "hid_ready", "down_ps", "summed"))

        block = ctx.enter_context(nc.Block())

        FIRST, LAST = UNITS, STEPS - 3 * UNITS

        @block.sync
        def _(sp):
            for b in range(B):
                for e in range(2):
                    sp.sem_inc(k_out[b][e], 1)
            sp.dma_start(ctx_buf[:, 0], ctx_in[0]).then_inc(ctx_in_s[0], 16)
            sp.dma_start(w_k[:], wk).then_inc(wk_in, 16)
            sp.dma_start(w_v[:], wv).then_inc(wv_in, 16)
            sp.dma_start(ctx_buf[:, 1], ctx_in[1]).then_inc(ctx_in_s[1], 16)
            sp.dma_start(xs[:], x.rearrange("(t p) e -> p t e", p=P)).then_inc(x_in, 16)
            sp.dma_start(w_q[:], wq).then_inc(wq_in, 16)
            sp.dma_start(raw_q, mask_q.rearrange("(t p) k -> p t k", p=P)).then_inc(mask_in, 16)
            sp.dma_start(raw_k, mask_k.rearrange("(t p) q -> p t q", p=P)).then_inc(mask_in, 16)
            sp.dma_start(w_o[:], wo).then_inc(wo_in, 16)
            sp.dma_start(bias_qk[:, 0, :], bq).then_inc(small_in, 16)
            sp.dma_start(bias_qk[:, 1, :], bk).then_inc(small_in, 16)
            sp.dma_start(bias_v[:], bv.rearrange("(o e) -> o e", o=1)).then_inc(small_in, 16)
            sp.dma_start(w_g[:], gate_w.rearrange("(a p) n -> p a n", p=P)).then_inc(small_in, 16)

            def store_k(b, i, j):
                for e in range(2):
                    sp.wait_ge(kl_ready[e], i * 2 + (NC * b + j + 2))
                    rows = k_parts[:, b * H + e * 8:b * H + e * 8 + 8].rearrange("a h d k -> (h d) a k")
                    sp.dma_start(rows[:, :, bass.ds((i * 2 + j) * CK, CK)], kp[:, e]).then_inc(k_out[b][e], 16)

            def load_chunk(b, i, j):
                sp.wait_ge(v_ps, i * 4 + 2 * (NC * b + j + 1))
                sp.dma_start(ctx_buf[:, j], ctx_in[i * 2 + (NC * b + j + 2)]).then_inc(ctx_in_s[j], 16)

            def load_stacks(n, slot):
                sp.dma_start(kst[0:48, slot, :], k_parts[0:3, n]).then_inc(stack_in[slot], 16)
                sp.dma_start(kst[48:80, slot, :], k_parts[0:2, n]).then_inc(stack_in[slot], 16)
                sp.dma_start(kst[80:96, slot, :], k_parts[0, n]).then_inc(stack_in[slot], 16)
                sp.dma_start(qst[0:48, slot, :], q_parts[0:1, n].broadcast_to([3, D, Q])).then_inc(stack_in[slot], 16)
                sp.dma_start(qst[48:80, slot, :], q_parts[1:2, n].broadcast_to([2, D, Q])).then_inc(stack_in[slot], 16)
                sp.dma_start(qst[80:96, slot, :], q_parts[2, n]).then_inc(stack_in[slot], 16)

            with sp.Fori(0, NC // 2) as i:
                for j in range(2):
                    store_k(0, i, j)
                    load_chunk(0, i, j)
            for e in range(KIN):
                sp.wait_ge(q_split, e + 1)
                for a in range(PARTS):
                    to = q_parts[a].rearrange("(b h) d q -> (h d) b q", b=B)[e * P:(e + 1) * P]
                    sp.dma_start(to, qp[:, a, e, :].rearrange("p (b q) -> p b q", b=B)).then_inc(q_out, 16)
            sp.wait_ge(q_out, 16 * PARTS * KIN)
            for e in range(2):
                sp.wait_ge(k_out[0][e], 16 * NC + 1)
            for n in range(2):
                load_stacks(n, n)
            with sp.Fori(0, NC // 2 - 1) as i:
                for j in range(2):
                    store_k(1, i, j)
                    load_chunk(1, i, j)
            for j in range(2):
                store_k(1, NC // 2 - 1, j)
            sp.wait_ge(v_ps, 2 * B * NC)
            for e in range(2):
                sp.wait_ge(k_out[1][e], 16 * NC + 1)
            for n in range(2, SLOTS):
                load_stacks(n, n)
            sp.dma_start(w_q[:], sq).then_inc(self_in, 16)
            sp.dma_start(w_k[:], sk).then_inc(self_in, 16)
            sp.dma_start(w_v[:], sv).then_inc(self_in, 16)
            with sp.Fori(0, NH // SLOTS - 1) as i:
                for slot in range(SLOTS):
                    n = sp.snap(i * SLOTS + (SLOTS + slot))
                    sp.wait_ge(b_ps, i * (SLOTS * UNITS) + (slot + 1) * UNITS)
                    load_stacks(n, slot)

            def load_up(e, s):
                sp.dma_start(up_sb[:, s], up_w[e]).then_inc(up_in[s], 16)

            def load_down(e, s):
                sp.dma_start(down_sb[:, s], down_w[e].rearrange("(a p) n -> p a n", p=P)).then_inc(down_in[s], 16)

            sp.wait_ge(vh_ready, H)
            for e in range(2):
                load_up(e, e)
                load_down(e, e)
            with sp.Fori(0, NE // 2 - 1) as i:
                for s in range(2):
                    e = sp.snap(i * 2 + (s + 2))
                    sp.wait_ge(up_ps, i * (2 * FT) + (s + 1) * FT)
                    load_up(e, s)
                    sp.wait_ge(down_ps, i * (2 * T) + (s + 1) * T)
                    load_down(e, s)
            sp.wait_ge(summed, NE * T + 1)
            sp.dma_start(out.rearrange("(t p) e -> p t e", p=P), xs[:]).then_inc(out_done, 16)
            sp.wait_ge(out_done, 16)

        @block.gpsimd
        def _(pool):
            for e in range(2):
                pool.sem_inc(kl_ready[e], 1)
            pool.memset(neg_half[:], -0.5).then_inc(pool_consts, 1)
            pool.memset(ident[:], 0.0).then_inc(pool_consts, 1)
            pool.memset(fold[:], 0.0).then_inc(pool_consts, 1)
            pool.memset(group_bias[:], 0.0).then_inc(pool_consts, 1)
            pool.wait_ge(pool_consts, 4)
            pool.affine_select(out=ident[:], in_=ident[:], compare_op=ALU.not_equal, fill=1.0, base=0,
                               pattern=[[-1, P]], channel_multiplier=1).then_inc(consts, 1)

            def rstds(n):
                pool.wait_ge(var_ready, n + 1)
                pool.tensor_tensor(rstd[:], var_eps[:], neg_half[:], ALU.pow).then_inc(rstd_ready, 1)

            rstds(0)
            for g in range(4):
                pool.affine_select(out=fold[:], in_=fold[:], compare_op=ALU.not_equal, fill=1.0, base=-32 * g,
                                   pattern=[[-1, 32]], channel_multiplier=1).then_inc(pool_consts, 1)
                pool.wait_ge(pool_consts, 5 + g)
            pool.affine_select(out=group_bias[:], in_=group_bias[:], compare_op=ALU.is_ge, fill=-BIG, base=0,
                               pattern=[[-GROUP, P // GROUP], [0, GROUP]], channel_multiplier=1).then_inc(pool_consts, 1)
            pool.wait_ge(pool_consts, 9)
            pool.affine_select(out=group_bias[:], in_=group_bias[:], compare_op=ALU.is_ge, fill=-BIG, base=GROUP - 1,
                               pattern=[[GROUP, P // GROUP], [0, GROUP]], channel_multiplier=-1).then_inc(consts, 1)
            pool.wait_ge(consts, 3)
            pool.memset(kst[STACK:ROWS, 0:2, :], 1.0).then_inc(ones_set, 1)
            pool.wait_ge(ones_set, 1)

            for b in range(B):
                with pool.Fori(0, NC // 2) as i:
                    for j in range(2):
                        for e in range(2):
                            pool.wait_ge(km_ready, i * 4 + (2 * NC * b + 2 * j + e + 1))
                            pool.tensor_tensor(kp[:, e, 2, :], rest[:, e, :], kp[:, e, 1, :],
                                               ALU.subtract).then_inc(kl_ready[e], 1)
            pool.wait_ge(v_ps, 2 * B * NC)
            for e in range(2):
                pool.wait_ge(k_out[1][e], 16 * NC + 1)
            pool.memset(kst[STACK:ROWS, 2:4, :], 1.0).then_inc(ones_set, 1)
            pool.wait_ge(ones_set, 2)

            pool.wait_ge(masks_ready, 2)
            with pool.Fori(0, NH) as n:
                for u in range(UNITS):
                    if u in POOL_UNITS:
                        pool.wait_ge(exp_done, n * UNITS + (u + 1))
                        tile = probs[:, u % 4, :]
                        keep = mask_int[:, POOL_UNITS.index(u)].rearrange("p k q -> p (k q)")
                        pool.tensor_tensor(tile.bitcast(I32), tile.bitcast(I32), keep, ALU.mult).then_inc(pool_masked, 1)
            rstds(1)
            rstds(2)

        @block.scalar
        def _(act):
            act.wait_ge(consts, 1)
            act.activation(ident_bf[:], ident[:], ACT.Copy).then_inc(consts, 1)

            def split_k(b):
                with act.Fori(0, NC // 2) as i:
                    for j in range(2):
                        for e in range(2):
                            act.wait_ge(k_ps, i * 4 + (2 * NC * b + 2 * j + e + 1))
                            act.wait_ge(k_out[b][e], i * 32 + (16 * j + 1))
                            act.activation(kp[:, e, 0, :], BANK[2 * j + e], ACT.Copy).then_inc(kh_ready, 1)
                        for e in range(2):
                            act.wait_ge(k_rest[j], i * 2 + (NC * b + e + 2))
                            act.activation(kp[:, e, 1, :], rest[:, e, :], ACT.Copy).then_inc(km_ready, 1)

            split_k(0)

            def copy_xnT(n, first_bank):
                for t in range(T):
                    act.wait_ge(xnT_ps, T * n + t + 1)
                    act.activation(xnT[:, :, t * P:(t + 1) * P],
                                   BANK[first_bank + t][:, 0:E].rearrange("p (a q) -> p a q", a=KIN),
                                   ACT.Copy).then_inc(xnT_ready, 1)

            copy_xnT(0, 0)
            for e in range(KIN):
                act.wait_ge(q_ps, e + 1)
                if e == 0:
                    act.wait_ge(k_out[0][0], 16 * NC + 1)
                act.activation(qp[:, 0, e, :], BANK[4 + e], ACT.Copy, scale=float(D) ** -0.5).then_inc(q_high, 1)
            for e in range(2):
                act.wait_ge(k_out[0][e], 16 * NC + 1)
            split_k(1)

            def copy_vh(n, p):
                act.activation(Vh[:, p, :, 0:D], V[:, n], ACT.Copy).then_inc(vh_ready, 1)

            def exp_unit(base, g):
                act.wait_ge(b_ps, base + g + 1)
                if g >= 4:
                    act.wait_ge(pv_done, base + (g - 3))
                act.activation(probs[:, g % 4, :], ps_b[:, g % 2, :], ACT.Exp).then_inc(exp_done, 1)

            def copy_rows(base, n):
                act.wait_ge(rows_ps, base + n + 1)
                act.activation(qst[STACK:ROWS, n % SLOTS, :], max_rows, ACT.Copy).then_inc(rows_ready, 1)

            def copy_oT(base, n):
                act.wait_ge(pv_done, base * UNITS + UNITS * (n + 1))
                if n >= 2:
                    act.wait_ge(o_ps, base + (n - 1))
                act.activation(oT[:, n % 2, :], ps_v[:, 0:Q], ACT.Copy).then_inc(oT_ready, 1)

            for b in range(2):
                act.wait_ge(v_stored[b], 2 * NC + 1)
            act.wait_ge(dve_consts, 2)
            act.wait_ge(masks_ready, 2)
            copy_vh(0, 0)
            copy_rows(0, 0)
            for g in range(LEAD_B):
                exp_unit(0, g)

            def step(base, heads, s):
                if s % UNITS == 0 and s > 0:
                    copy_oT(heads, s // UNITS - 1)
                if s % UNITS == 4 and s // UNITS + 1 < NH:
                    copy_rows(heads, s // UNITS + 1)
                if s + LEAD_B < STEPS:
                    exp_unit(base, s + LEAD_B)
                if s % UNITS == 6 and s // UNITS + 1 < NH:
                    n = s // UNITS + 1
                    if n >= 2:
                        act.wait_ge(pv_done, base + UNITS * (n - 1))
                    copy_vh(heads + n, n % 2)

            for s in range(FIRST):
                step(0, 0, s)
            body = SLOTS * UNITS
            with act.Fori(0, (LAST - FIRST) // body) as i:
                for s in range(FIRST, FIRST + body):
                    step(i * body, i * SLOTS, s)
            for s in range(LAST, STEPS):
                step(0, 0, s)
            copy_oT(0, NH - 1)

            for t in range(T):
                act.wait_ge(aT_ps, t + 1)
                act.activation(aT[:, t, :], BANK[t][:, 0:E], ACT.Copy).then_inc(aT_ready, 1)
            copy_xnT(1, 0)
            act.wait_ge(small_in, 64)
            for m, to in enumerate((q2T, k2T)):
                for e in range(KIN):
                    act.wait_ge(qk2_ps, 2 * m + e + 1)
                    act.activation(to[:, e, :], BANK[4 + 2 * m + e], ACT.Identity,
                                   bias=bias_qk[:, m, e:e + 1]).then_inc(qk2_ready, 1)
            for t in range(T):
                act.wait_ge(s2_ready, t + 1)
                act.activation(p2[:, t, :], s2[:, t, :], ACT.Exp, bias=tk[:, 1, t:t + 1],
                               accum_out=tk[:, 2, t:t + 1]).then_inc(p2_ready, 1)
            for t in range(T):
                act.wait_ge(p2T_ps, t + 1)
                act.activation(p2T[:, t, :], BANK[t][:, 256:384], ACT.Copy).then_inc(p2T_ready, 1)
            copy_xnT(2, 0)
            act.wait_ge(gate_sub, 1)
            act.activation(lg[:, 1], lg[:, 0], ACT.Exp).then_inc(gate_exp, 1)

            def gates(base, e):
                for f in range(FT):
                    act.wait_ge(up_ps, base * FT + (FT * e + f + 1))
                    act.activation(silu[:, f % 2, :], BANK[2 * (f % 2)], ACT.Silu).then_inc(silu_ready, 1)

            gates(0, 0)
            with act.Fori(0, NE // 2 - 1) as i:
                for j in range(2):
                    gates(i * 2, j + 1)
            gates(0, NE - 1)

        @block.vector
        def _(dve):
            count = [0]

            def link(ins):
                count[0] += 1
                ins.then_inc(dve_own, 1)
                dve.wait_ge(dve_own, count[0])

            def mark(ins):
                count[0] += 1
                ins.then_inc(dve_own, 1)

            def layer_norm(n):
                for t in range(T):
                    mark(dve.bn_stats(stats[:, t, :], xs[:, t, :]))
                dve.wait_ge(dve_own, count[0])
                for t in range(T):
                    mark(dve.bn_aggr(mean_var[:, t, :], stats[:, t, :]))
                dve.wait_ge(dve_own, count[0])
                dve.tensor_scalar(var_eps[:], mean_var[:, :, 1], EPS, None, ALU.add).then_inc(var_ready, 1)
                dve.wait_ge(rstd_ready, n + 1)
                for t in range(T):
                    dve.tensor_scalar(xn[:, t, :], xs[:, t, :], mean_var[:, t, 0:1], rstd[:, t:t + 1],
                                      ALU.subtract, ALU.mult).then_inc(xn_ready, 1)

            for j in range(2):
                dve.sem_inc(k_rest[j], 1)
                dve.sem_inc(v_stored[j], 1)
            dve.sem_inc(summed, 1)
            dve.wait_ge(x_in, 16)
            layer_norm(0)

            def store_kv(b):
                with dve.Fori(0, NC // 2) as i:
                    for j in range(2):
                        for e in range(2):
                            dve.wait_ge(kh_ready, i * 4 + (2 * NC * b + 2 * j + e + 1))
                            dve.wait_ge(kl_ready[e], i * 2 + (NC * b + j + 1))
                            dve.tensor_tensor(rest[:, e, :], BANK[2 * j + e], kp[:, e, 0, :],
                                              ALU.subtract).then_inc(k_rest[j], 1)
                        for v in range(2):
                            dve.wait_ge(v_ps, i * 4 + (2 * NC * b + 2 * j + v + 1))
                            to = V[:, b * H:(b + 1) * H, bass.ds(i * 8 + (4 * j + 2 * v), 2), :]
                            dve.tensor_copy(to, BANK[4 + 2 * j + v].rearrange("p (k h d) -> p h k d", k=2, h=H)
                                            ).then_inc(v_stored[j], 1)

            store_kv(0)
            for e in range(KIN):
                dve.wait_ge(q_high, e + 1)
                dve.wait_ge(kl_ready[e], NC + 1)
                rest_q = rest[:, e, :]
                link(dve.scalar_tensor_tensor(rest_q, BANK[4 + e], float(D) ** -0.5, qp[:, 0, e, :],
                                              ALU.mult, ALU.subtract))
                link(dve.tensor_copy(qp[:, 1, e, :], rest_q))
                dve.tensor_tensor(qp[:, 2, e, :], rest_q, qp[:, 1, e, :], ALU.subtract).then_inc(q_split, 1)
            dve.wait_ge(mask_in, 32)
            for t in range(Q // P):
                ins = dve.tensor_scalar(mask_bias[:, t, :], raw_q[:, t, :], BIG, -BIG, ALU.mult, ALU.add)
            ins.then_inc(masks_ready, 1)
            for u in range(UNITS):
                keys = raw_k[:, u * UT:(u + 1) * UT, :]
                if u in PE_UNITS:
                    ins = dve.tensor_scalar(mask_turned[:, PE_UNITS.index(u)], keys, BIG, -BIG, ALU.mult, ALU.add)
                else:
                    ins = dve.tensor_copy(mask_int[:, POOL_UNITS.index(u)], keys)
            ins.then_inc(masks_ready, 1)
            dve.memset(Vh[:], 0.0).then_inc(dve_consts, 1)
            dve.wait_ge(dve_consts, 1)
            dve.memset(Vh[:, :, :, D:D + 1], 1.0).then_inc(dve_consts, 1)
            for n in range(NE):
                ins = dve.memset(rank[:, n:n + 1], float(NE - n))
            mark(ins)
            mark(dve.memset(ones_row[:], 1.0))
            dve.wait_ge(q_out, 16 * PARTS * KIN)
            store_kv(1)

            def maxima(base, a):
                u, n = a % UNITS, a // UNITS
                for t in range(2):
                    dve.wait_ge(a_ps, base * 2 + (2 * a + t + 1))
                    dve.sem_inc(tiles_seen, 1)
                    dve.tensor_tensor_reduce(unused[:, t, :], ps_a[:, t, :], mask_bias[:, t, u * UK:(u + 1) * UK],
                                             1.0, -BIG, ALU.add, ALU.max,
                                             unit_max[:, n % 2, t, u:u + 1]).then_inc(a_max, 1)

            def negate_max(heads, n):
                p = n % 2
                dve.wait_ge(a_max, heads * 16 + 16 * (n + 1))
                dve.tensor_reduce(head_max[:, p, :], unit_max[:, p], AX, ALU.max).then_inc(chain, 1)
                dve.wait_ge(chain, heads * 4 + (4 * n + 1))
                dve.tensor_scalar(any_kept[:, heads + n, :], head_max[:, p, :], -1e38, None, ALU.is_gt)
                dve.tensor_scalar(neg_parts[:, p, :, 0], head_max[:, p, :], -1.0, None, ALU.mult).then_inc(chain, 1)
                dve.wait_ge(chain, heads * 4 + (4 * n + 2))
                dve.scalar_tensor_tensor(neg_rest[:, p, :], head_max[:, p, :], -1.0, neg_parts[:, p, :, 0],
                                         ALU.mult, ALU.subtract).then_inc(chain, 1)
                dve.wait_ge(chain, heads * 4 + (4 * n + 3))
                dve.tensor_copy(neg_parts[:, p, :, 1], neg_rest[:, p, :]).then_inc(chain, 1)
                dve.wait_ge(chain, heads * 4 + (4 * n + 4))
                dve.tensor_tensor(neg_parts[:, p, :, 2], neg_rest[:, p, :], neg_parts[:, p, :, 1],
                                  ALU.subtract).then_inc(neg_ready, 1)

            def store_o(heads, n):
                dve.wait_ge(o_ps, heads + n + 1)
                dve.tensor_copy(O[:, heads + n, :, :], o_cols[:, :, 0:D + 1]).then_inc(o_stored, 1)

            for a in range(UNITS):
                maxima(0, a)
            negate_max(0, 0)
            for a in range(UNITS, LEAD_A):
                maxima(0, a)

            def step(base, heads, s):
                if s + LEAD_A < STEPS:
                    maxima(base, s + LEAD_A)
                if s % UNITS == 1 and s // UNITS + 1 < NH:
                    negate_max(heads, s // UNITS + 1)
                if s % UNITS == 3 and s >= UNITS:
                    store_o(heads, s // UNITS - 1)

            for s in range(FIRST):
                step(0, 0, s)
            with dve.Fori(0, (LAST - FIRST) // (2 * UNITS)) as i:
                for s in range(FIRST, FIRST + 2 * UNITS):
                    step(i * (2 * UNITS), i * 2, s)
            for s in range(LAST, STEPS):
                step(0, 0, s)
            store_o(0, NH - 1)
            dve.wait_ge(o_stored, NH)

            link(dve.tensor_tensor(norm[:], O[:, :, :, D], any_kept[:], ALU.mult))
            link(dve.reciprocal(norm[:], norm[:]))
            link(dve.tensor_tensor(norm[:], norm[:], any_kept[:], ALU.mult))
            for b in range(B):
                for t in range(2):
                    dve.tensor_tensor(attn[:, 2 * b + t, :].rearrange("p (h d) -> p h d", h=H),
                                      O[:, b * H:(b + 1) * H, t, 0:D],
                                      norm[:, b * H:(b + 1) * H, t:t + 1].broadcast_to([P, H, D]),
                                      ALU.mult).then_inc(attn_ready, 1)
            for t in range(T):
                dve.wait_ge(wo_ps, t + 1)
                mark(dve.tensor_tensor(xs[:, t, :], xs[:, t, :], BANK[4 + t][:, 0:E], ALU.add))
            dve.wait_ge(dve_own, count[0])
            layer_norm(1)
            for t in range(T):
                dve.wait_ge(v2_ps, t + 1)
                dve.tensor_copy(v2[:, t, :], BANK[t][:, 0:E]).then_inc(v2_ready, 1)
            group_b = group_bias[:].rearrange("p a b -> p (a b)")
            dve.wait_ge(consts, 3)
            for t in range(T):
                dve.wait_ge(s2_ps, t + 1)
                link(dve.tensor_tensor_reduce(s2[:, t, :], BANK[4 + t][:, 0:P], group_b, 1.0, -BIG,
                                              ALU.add, ALU.max, tk[:, 0, t:t + 1]))
                dve.tensor_scalar(tk[:, 1, t:t + 1], tk[:, 0, t:t + 1], -1.0, None, ALU.mult).then_inc(s2_ready, 1)
            dve.wait_ge(p2_ready, T)
            link(dve.reciprocal(tk[:, 3, :], tk[:, 2, :]))
            for t in range(T):
                dve.wait_ge(o2_ps, t + 1)
                mark(dve.scalar_tensor_tensor(xs[:, t, :], BANK[4 + t][:, 256:512], tk[:, 3, t:t + 1], xs[:, t, :],
                                              ALU.mult, ALU.add))
            dve.wait_ge(dve_own, count[0])
            layer_norm(2)

            def wide(col):
                return col.rearrange("p (t o) -> p t o", o=1).broadcast_to([P, T, NE])

            ranks = rank[:].rearrange("p (o n) -> p o n", o=1).broadcast_to([P, T, NE])
            logits = ps_m[:, 0:T * NE].rearrange("p (t n) -> p t n", t=T)
            dve.wait_ge(gate_ps, 1)
            link(dve.tensor_reduce(tk[:, 4, :], logits, AX, ALU.max))
            dve.tensor_tensor(lg[:, 0], logits, wide(tk[:, 4, :]), ALU.subtract).then_inc(gate_sub, 1)
            dve.wait_ge(gate_exp, 1)
            link(dve.tensor_reduce(tk[:, 5, :], lg[:, 1], AX, ALU.add))
            link(dve.reciprocal(tk[:, 5, :], tk[:, 5, :]))
            link(dve.tensor_tensor(lg[:, 2], lg[:, 1], wide(tk[:, 5, :]), ALU.mult))

            def pick(values, best, chosen):
                link(dve.tensor_reduce(tk[:, best, :], values, AX, ALU.max))
                link(dve.tensor_tensor(lg[:, 3], values, wide(tk[:, best, :]), ALU.is_equal))
                link(dve.tensor_tensor(lg[:, 3], lg[:, 3], ranks, ALU.mult))
                link(dve.tensor_reduce(tk[:, 4, :], lg[:, 3], AX, ALU.max))
                link(dve.tensor_tensor(chosen, lg[:, 3], wide(tk[:, 4, :]), ALU.is_equal))

            pick(lg[:, 2], 6, lg[:, 4])
            link(dve.scalar_tensor_tensor(lg[:, 5], lg[:, 4], -2.0, lg[:, 2], ALU.mult, ALU.add))
            pick(lg[:, 5], 7, lg[:, 6])
            link(dve.tensor_tensor(tk[:, 5, :], tk[:, 6, :], tk[:, 7, :], ALU.add))
            link(dve.reciprocal(tk[:, 5, :], tk[:, 5, :]))
            link(dve.tensor_tensor(lg[:, 4], lg[:, 4], lg[:, 6], ALU.add))
            link(dve.tensor_tensor(lg[:, 4], lg[:, 4], lg[:, 2], ALU.mult))
            link(dve.tensor_tensor(wgt[:].rearrange("p n t -> p t n"), lg[:, 4], wide(tk[:, 5, :]), ALU.mult))

            def hidden(base, e):
                for f in range(FT):
                    dve.wait_ge(silu_ready, base * FT + (FT * e + f + 1))
                    dve.tensor_tensor(hid[:, e % 2, f, :], silu[:, f % 2, :], BANK[2 * (f % 2) + 1],
                                      ALU.mult).then_inc(hid_ready, 1)

            def add_expert(base, e):
                for t in range(T):
                    dve.wait_ge(down_ps, base * T + (T * e + t + 1))
                    dve.scalar_tensor_tensor(xs[:, t, :], BANK[4 + t][:, 0:E], wgt[:, base + e, t:t + 1],
                                             xs[:, t, :], ALU.mult, ALU.add).then_inc(summed, 1)

            hidden(0, 0)
            with dve.Fori(0, NE // 2 - 1) as i:
                for j in range(2):
                    hidden(i * 2, j + 1)
                    add_expert(i * 2, j)
            hidden(0, NE - 1)
            add_expert(0, NE - 2)
            add_expert(0, NE - 1)

        @block.tensor
        def _(pe):
            def transpose_xn(n, first_bank):
                for t in range(T):
                    pe.wait_ge(xn_ready, T * n + t + 1)
                    for a in range(KIN):
                        ins = pe.transpose(BANK[first_bank + t][:, a * P:(a + 1) * P], xn[:, t, a * P:(a + 1) * P],
                                           ident[:])
                    ins.then_inc(xnT_ps, 1)

            def project_kv(b):
                with pe.Fori(0, NC // 2) as i:
                    for j in range(2):
                        pe.wait_ge(ctx_in_s[j], i * 16 + 16 * (NC // 2 * b + 1))
                        pe.wait_ge(k_rest[j], i * 2 + (NC * b + 1))
                        for e in range(2):
                            for a in range(KIN):
                                ins = pe.matmul(BANK[2 * j + e], w_k[:, a, e * P:(e + 1) * P], ctx_buf[:, j, a, :],
                                                start=(a == 0), stop=(a == KIN - 1))
                            ins.then_inc(k_ps, 1)
                        pe.wait_ge(v_stored[j], i * 2 + (NC * b + 1))
                        for v in range(2):
                            for k in range(2):
                                for a in range(KIN):
                                    key = (2 * v + k) * P
                                    ins = pe.matmul(BANK[4 + 2 * j + v][:, k * E:(k + 1) * E],
                                                    ctx_buf[:, j, a, key:key + P], w_v[:, a, :],
                                                    start=(a == 0), stop=(a == KIN - 1))
                            ins.then_inc(v_ps, 1)

            pe.wait_ge(wk_in, 16)
            pe.wait_ge(wv_in, 16)
            pe.wait_ge(consts, 1)
            project_kv(0)
            for j in range(2):
                pe.wait_ge(k_rest[j], NC + 1)
                pe.wait_ge(v_stored[j], NC + 1)
            transpose_xn(0, 0)
            pe.wait_ge(wq_in, 16)
            pe.wait_ge(xnT_ready, T)
            for e in range(KIN):
                for a in range(KIN):
                    ins = pe.matmul(BANK[4 + e], w_q[:, a, e * P:(e + 1) * P], xnT[:, a, :],
                                    start=(a == 0), stop=(a == KIN - 1))
                ins.then_inc(q_ps, 1)
            pe.wait_ge(q_split, KIN)
            project_kv(1)

            def scores_for_max(base, a):
                n, u = a // UNITS, a % UNITS
                slot = n % SLOTS
                if u == 0:
                    pe.wait_ge(stack_in[slot], base * (16 * LOADS // (SLOTS * UNITS)) + 16 * LOADS * (n // SLOTS + 1))
                for t in range(2):
                    if a >= 1:
                        pe.wait_ge(a_max, base * 2 + (2 * a + t - 1))
                    pe.matmul(ps_a[:, t, :], qst[0:STACK, slot, t * P:(t + 1) * P],
                              kst[0:STACK, slot, u * UK:(u + 1) * UK], start=True, stop=True).then_inc(a_ps, 1)

            def turn_max(heads, n):
                pe.wait_ge(neg_ready, heads + n + 1)
                if n >= 2:
                    pe.wait_ge(o_stored, heads + (n - 1))
                for t in range(2):
                    ins = pe.matmul(ps_m[STACK:STACK + PARTS, t * P:(t + 1) * P], neg_parts[:, n % 2, t, 0:PARTS],
                                    ident_bf[:], start=True, stop=True)
                ins.then_inc(rows_ps, 1)

            def scores(base, heads, g):
                n, u = g // UNITS, g % UNITS
                slot = n % SLOTS
                if u == 0:
                    pe.wait_ge(rows_ready, heads + n + 1)
                if g >= 2:
                    pe.wait_ge(exp_done, base + (g - 1))
                if u in PE_UNITS:
                    bias = mask_turned[:, PE_UNITS.index(u)].rearrange("p k q -> p (k q)")
                    for c in range(2):
                        pe.matmul(ps_b[:, g % 2, c * 512:(c + 1) * 512], ident_bf[:],
                                  bias[:, c * 512:(c + 1) * 512], start=True, stop=False, skip_group_check=True)
                for k in range(UT):
                    key = u * UK + k * P
                    ins = pe.matmul(ps_b[:, g % 2, k * Q:(k + 1) * Q], kst[0:ROWS, slot, key:key + P],
                                    qst[0:ROWS, slot, :], start=u not in PE_UNITS, stop=True,
                                    skip_group_check=u in PE_UNITS)
                ins.then_inc(b_ps, 1)

            def values(base, heads, g):
                n, u = g // UNITS, g % UNITS
                if u in POOL_UNITS:
                    masked = n * len(POOL_UNITS) + POOL_UNITS.index(u) + 1
                    pe.wait_ge(pool_masked, heads * len(POOL_UNITS) + masked)
                else:
                    pe.wait_ge(exp_done, base + (g + 1))
                if u == 0:
                    pe.wait_ge(vh_ready, heads + n + 1)
                    if n >= 1:
                        pe.wait_ge(oT_ready, heads + n)
                for k in range(UT):
                    ins = pe.matmul(ps_v[32 * k:32 * k + 32, 0:Q], Vh[:, n % 2, u * UT + k, :],
                                    probs[:, g % 4, k * Q:(k + 1) * Q], start=(u == 0), stop=(u == UNITS - 1))
                ins.then_inc(pv_done, 1)

            def fold_o(heads, n):
                pe.wait_ge(oT_ready, heads + n + 1)
                for t in range(2):
                    ins = pe.matmul(o_cols[:, t, 0:D + 1], oT[:, n % 2, t * P:(t + 1) * P], fold[:, 0:D + 1],
                                    start=True, stop=True)
                ins.then_inc(o_ps, 1)

            for j in range(2):
                pe.wait_ge(k_rest[j], B * NC + 1)
                pe.wait_ge(v_stored[j], B * NC + 1)
            pe.wait_ge(masks_ready, 2)
            pe.wait_ge(consts, 3)
            pe.wait_ge(ones_set, 2)
            for a in range(UNITS):
                scores_for_max(0, a)
            turn_max(0, 0)
            for a in range(UNITS, LEAD_A):
                scores_for_max(0, a)
            for g in range(LEAD_B):
                scores(0, 0, g)

            def step(base, heads, s):
                n = s // UNITS
                if s + LEAD_A < STEPS:
                    scores_for_max(base, s + LEAD_A)
                if s % UNITS == 2 and s >= UNITS:
                    fold_o(heads, n - 1)
                if s % UNITS == 4 and n + 1 < NH:
                    turn_max(heads, n + 1)
                if s + LEAD_B < STEPS:
                    scores(base, heads, s + LEAD_B)
                values(base, heads, s)

            for s in range(FIRST):
                step(0, 0, s)
            body = SLOTS * UNITS
            with pe.Fori(0, (LAST - FIRST) // body) as i:
                for s in range(FIRST, FIRST + body):
                    step(i * body, i * SLOTS, s)
            for s in range(LAST, STEPS):
                step(0, 0, s)
            pe.wait_ge(o_stored, NH - 1)
            fold_o(0, NH - 1)

            pe.wait_ge(wo_in, 16)
            for t in range(T):
                pe.wait_ge(attn_ready, t + 1)
                for a in range(KIN):
                    ins = pe.transpose(BANK[t][:, a * P:(a + 1) * P], attn[:, t, a * P:(a + 1) * P], ident[:])
                ins.then_inc(aT_ps, 1)
            for t in range(T):
                pe.wait_ge(aT_ready, t + 1)
                for a in range(KIN):
                    ins = pe.matmul(BANK[4 + t][:, 0:E], aT[:, t, a * P:(a + 1) * P], w_o[:, a, :],
                                    start=(a == 0), stop=(a == KIN - 1))
                ins.then_inc(wo_ps, 1)
            transpose_xn(1, 0)
            pe.wait_ge(self_in, 48)
            pe.wait_ge(xnT_ready, 2 * T)
            for m, w in enumerate((w_q, w_k)):
                for e in range(KIN):
                    for a in range(KIN):
                        ins = pe.matmul(BANK[4 + 2 * m + e], w[:, a, e * P:(e + 1) * P], xnT[:, a, :],
                                        start=(a == 0), stop=(a == KIN - 1))
                    ins.then_inc(qk2_ps, 1)
            pe.wait_ge(small_in, 64)
            for t in range(T):
                for a in range(KIN):
                    pe.matmul(BANK[t][:, 0:E], xnT[:, a, t * P:(t + 1) * P], w_v[:, a, :], start=(a == 0), stop=False)
                pe.matmul(BANK[t][:, 0:E], ones_row[:], bias_v[:], start=False, stop=True).then_inc(v2_ps, 1)
            pe.wait_ge(qk2_ready, 2 * KIN)
            for t in range(T):
                for e in range(KIN):
                    ins = pe.matmul(BANK[4 + t][:, 0:P], q2T[:, e, t * P:(t + 1) * P], k2T[:, e, t * P:(t + 1) * P],
                                    start=(e == 0), stop=(e == KIN - 1))
                ins.then_inc(s2_ps, 1)
            for t in range(T):
                pe.wait_ge(p2_ready, t + 1)
                pe.wait_ge(v2_ready, t + 1)
                pe.transpose(BANK[t][:, 256:384], p2[:, t, :], ident[:]).then_inc(p2T_ps, 1)
            for t in range(T):
                pe.wait_ge(p2T_ready, t + 1)
                pe.matmul(BANK[4 + t][:, 256:512], p2T[:, t, :], v2[:, t, :], start=True, stop=True).then_inc(o2_ps, 1)
            transpose_xn(2, 0)
            pe.wait_ge(xnT_ready, 3 * T)
            for t in range(T):
                for a in range(KIN):
                    ins = pe.matmul(ps_m[:, t * NE:(t + 1) * NE], xnT[:, a, t * P:(t + 1) * P], w_g[:, a, :],
                                    start=(a == 0), stop=(a == KIN - 1))
            ins.then_inc(gate_ps, 1)

            def up(base, e):
                pe.wait_ge(up_in[e % 2], base * 8 + 16 * (e // 2 + 1))
                for f in range(FT):
                    if e or f >= 2:
                        pe.wait_ge(hid_ready, base * FT + (FT * e + f - 1))
                    for m in range(2):
                        for a in range(KIN):
                            col = m * F + f * P
                            ins = pe.matmul(BANK[2 * (f % 2) + m], up_sb[:, e % 2, a, col:col + P], xnT[:, a, :],
                                            start=(a == 0), stop=(a == KIN - 1))
                    ins.then_inc(up_ps, 1)

            def down(base, e):
                pe.wait_ge(hid_ready, base * FT + FT * (e + 1))
                pe.wait_ge(down_in[e % 2], base * 8 + 16 * (e // 2 + 1))
                pe.wait_ge(summed, base * T + (T * e + 1))
                for t in range(T):
                    for f in range(FT):
                        ins = pe.matmul(BANK[4 + t][:, 0:E], hid[:, e % 2, f, t * P:(t + 1) * P],
                                        down_sb[:, e % 2, f, :], start=(f == 0), stop=(f == FT - 1))
                    ins.then_inc(down_ps, 1)

            up(0, 0)
            pe.wait_ge(gate_sub, 1)
            with pe.Fori(0, NE // 2 - 1) as i:
                for j in range(2):
                    up(i * 2, j + 1)
                    down(i * 2, j)
            up(0, NE - 1)
            down(0, NE - 2)
            down(0, NE - 1)


def kernel(x, ctx_1024, mask_1x1xSxS2_bk0, L0_xattn_wq, L0_xattn_wk, L0_xattn_wv, L0_xattn_wo, L0_attn_Wq,
           L0_attn_bq, L0_attn_Wk, L0_attn_bk, L0_attn_Wv, L0_attn_bv, L0_ffn_gate_w, L0_ffn_gate_up_w,
           L0_ffn_down_w):
    import numpy as np
    import concourse.bacc as bacc
    from concourse.bass_utils import run_bass_kernel_spmd

    def turned(w):
        return np.asarray(w).T.reshape(KIN, P, E).transpose(1, 0, 2)

    mask = np.asarray(mask_1x1xSxS2_bk0).reshape(Q, S)
    chunks = np.asarray(ctx_1024).reshape(B * NC, CK, KIN, P).transpose(0, 3, 2, 1)
    ups = np.asarray(L0_ffn_gate_up_w).reshape(NE, KIN, P, 2 * F).transpose(0, 2, 1, 3)
    arrays = {
        "x": np.asarray(x).reshape(B * Q, E), "ctx_in": chunks, "mask_q": mask, "mask_k": mask.T,
        "wq": turned(L0_xattn_wq), "wk": turned(L0_xattn_wk), "wv": turned(L0_xattn_wv), "wo": turned(L0_xattn_wo),
        "sq": turned(L0_attn_Wq), "bq": np.asarray(L0_attn_bq).reshape(KIN, P).T, "sk": turned(L0_attn_Wk), "bk": np.asarray(L0_attn_bk).reshape(KIN, P).T,
        "sv": turned(L0_attn_Wv), "bv": L0_attn_bv,
        "gate_w": L0_ffn_gate_w, "up_w": ups, "down_w": L0_ffn_down_w,
    }
    arrays = {name: np.ascontiguousarray(a) for name, a in arrays.items()}
    nc = bacc.Bacc("TRN2", target_bir_lowering=False, num_devices=1)
    args = {name: nc.dram_tensor(name, a.shape, mybir.dt.from_np(a.dtype), kind="ExternalInput").ap()
            for name, a in arrays.items()}
    out = nc.dram_tensor("out", (B * Q, E), F32, kind="ExternalOutput").ap()
    perceiver_block(nc, out=out, **args)
    got = run_bass_kernel_spmd(nc, [arrays], core_ids=[0])
    return got.results[0]["out"].reshape(B, Q, E)
```

```python
from contextlib import ExitStack

import concourse.bass as bass
from concourse import mybir

F32 = mybir.dt.float32
F32R = mybir.dt.float32r
BF16 = mybir.dt.bfloat16
I32 = mybir.dt.int32
U8 = mybir.dt.uint8
ALU = mybir.AluOpType
ACT = mybir.ActivationFunctionType
AX = mybir.AxisListType.X

P = 128
B, Q, E, S = 2, 256, 256, 4096
H, D = 16, 16
NH = B * H
T = B * Q // P
KIN = E // P
CK = 512
NC = S // CK
KT = S // P
UNITS = 8
UK = S // UNITS
UT = UK // P
STEPS = NH * UNITS
GROUP = 16
NE, F = 8, 512
FT = F // P
PARTS = 3
STACK = 6 * D
ROWS = STACK + PARTS
LEAD_A = 14
LEAD_B = 3
PE_UNITS = (1, 3, 5)
DVE_UNITS = (7,)
POOL_UNITS = tuple(u for u in range(UNITS) if u not in PE_UNITS + DVE_UNITS)
INT_UNITS = POOL_UNITS + DVE_UNITS
MASK_SLICE = len(INT_UNITS) * UT * Q // NC
BIG = 3.0e38
EPS = 1e-5
SLOTS = 4
LOADS = 6


def perceiver_block(nc, x, ctx_in, mask_q, mask_k, wq, wk, wv, wo, sq, bq, sk, bk, sv, bv, gate_w, up_w, down_w, out):
    k_parts = nc.dram_tensor("k_parts", (PARTS, NH, D, S), BF16, kind="Internal").ap()
    q_parts = nc.dram_tensor("q_parts", (PARTS, NH, D, Q), BF16, kind="Internal").ap()

    with ExitStack() as ctx:
        def sb(name, shape, dt=F32):
            return ctx.enter_context(nc.sbuf_tensor(name, shape, dt))

        def sem(name):
            return ctx.enter_context(nc.semaphore(name))

        V = sb("V", [P, NH, KT, D])
        qst = sb("qst", [P, SLOTS, Q], BF16)
        xs = sb("xs", [P, T, E])
        xn = sb("xn", [P, T, E])
        xnT = sb("xnT", [P, KIN, B * Q])
        w_q = sb("w_q", [P, KIN, E])
        w_o = sb("w_o", [P, KIN, E])
        kp = sb("kp", [P, 2, 2, PARTS, CK], BF16)
        qp = sb("qp", [P, PARTS, KIN, B * Q], BF16)
        O = sb("O", [P, NH, Q // P, D + 1])
        norm = sb("norm", [P, NH, Q // P])
        any_kept = sb("any_kept", [P, NH, Q // P])
        ident = sb("ident", [P, P])
        ident_bf = sb("ident_bf", [P, P], BF16)
        fold = sb("fold", [P, 32])
        stats = sb("stats", [P, T, 6])
        mean_var = sb("mean_var", [P, T, 2])
        var_eps = sb("var_eps", [P, T])
        rstd = sb("rstd", [P, T])
        neg_half = sb("neg_half", [P, T])
        bias_qk = sb("bias_qk", [P, 2, KIN])
        bias_v = sb("bias_v", [1, E])
        ones_row = sb("ones_row", [1, P])
        group_bias = sb("group_bias", [P, P // GROUP, GROUP])
        w_g = sb("w_g", [P, KIN, NE])
        rank = sb("rank", [P, NE])
        lg = sb("lg", [P, 8, T, NE])
        tk = sb("tk", [P, 8, T])
        wgt = sb("wgt", [P, NE, T])

        with ExitStack() as phase:
            def of_phase(name, shape, dt=F32):
                return phase.enter_context(nc.sbuf_tensor(name, shape, dt))

            ctx_raw = of_phase("ctx_raw", [P, 2, KIN, CK])
            ctx_high = of_phase("ctx_high", [P, 2, KIN, CK], F32R)
            ctx_low = of_phase("ctx_low", [P, 2, KIN, CK], F32R)
            rest = of_phase("rest", [P, 2, CK])
            w_high = of_phase("w_high", [P, 2, KIN, E], F32R)
            w_low = of_phase("w_low", [P, 2, KIN, E], F32R)
        with ExitStack() as phase:
            def of_phase(name, shape, dt=F32):
                return phase.enter_context(nc.sbuf_tensor(name, shape, dt))

            kst_late = of_phase("kst_late", [P, 2, S], BF16)
            probs = of_phase("probs", [P, 4, UT * Q])
            Vh = of_phase("Vh", [P, 2, KT, 32])
            kst_early = of_phase("kst_early", [P, 2, S], BF16)
            mask_bias = of_phase("mask_bias", [P, Q // P, S], BF16)
            mask_turned = of_phase("mask_turned", [P, len(PE_UNITS), UT, Q], BF16)
            mask_int = of_phase("mask_int", [P, len(INT_UNITS), UT, Q], I32)
            unit_max = of_phase("unit_max", [P, 2, Q // P, UNITS])
            head_max = of_phase("head_max", [P, 2, Q // P])
            neg_parts = of_phase("neg_parts", [P, 2, Q // P, 4], BF16)
            neg_rest = of_phase("neg_rest", [P, 2, Q // P])
        kst = [kst_early[:, 0, :], kst_early[:, 1, :], kst_late[:, 0, :], kst_late[:, 1, :]]
        with ExitStack() as phase:
            def of_phase(name, shape, dt=F32):
                return phase.enter_context(nc.sbuf_tensor(name, shape, dt))

            xnT_high = of_phase("xnT_high", [P, KIN, B * Q], F32R)
            xnT_low = of_phase("xnT_low", [P, KIN, B * Q], F32R)
            up_high = of_phase("up_high", [P, 2, KIN, 2 * F], F32R)
            up_low = of_phase("up_low", [P, 2, KIN, 2 * F], F32R)
            down_high = of_phase("down_high", [P, 2, FT, E], F32R)
            down_low = of_phase("down_low", [P, 2, FT, E], F32R)
            hid_high = of_phase("hid_high", [P, 2, FT, B * Q], F32R)
            hid_low = of_phase("hid_low", [P, 2, FT, B * Q], F32R)

        V_flat = V[:].rearrange("p h k d -> p (h k d)")
        half = H * KT * D
        w_raw = V_flat[:, half:half + 2 * KIN * E].rearrange("p (w a n) -> p w a n", w=2, a=KIN)
        raw_q = V_flat[:, half + 2560:half + 4608].bitcast(U8).rearrange("p (t k) -> p t k", t=Q // P)
        raw_k = V_flat[:, half + 4608:half + 6656].bitcast(U8).rearrange("p (k q) -> p k q", k=KT)
        raw_k_flat = V_flat[:, half + 4608:half + 6656].bitcast(U8)
        mask_int_flat = mask_int[:].rearrange("p u k q -> p (u k q)")
        oT = w_q
        unused = qp[:, 0]
        up_sb = V_flat[:, 0:2 * KIN * 2 * F].rearrange("p (s a n) -> p s a n", s=2, a=KIN)
        down_sb = V_flat[:, 4096:4096 + 2 * FT * E].rearrange("p (s a n) -> p s a n", s=2, a=FT)
        self_w = V_flat[:, 6144:6144 + 3 * KIN * E].rearrange("p (w a n) -> p w a n", w=3, a=KIN)
        at = half
        q2T = V_flat[:, at:at + 1024].rearrange("p (a t) -> p a t", a=KIN)
        k2T = V_flat[:, at + 1024:at + 2048].rearrange("p (a t) -> p a t", a=KIN)
        v2 = V_flat[:, at + 2048:at + 3072].rearrange("p (t e) -> p t e", t=T)
        attn = V_flat[:, at + 3072:at + 4096].rearrange("p (t e) -> p t e", t=T)
        aT = V_flat[:, at + 4096:at + 5120].rearrange("p (t e) -> p t e", t=T)
        s2 = V_flat[:, at + 5120:at + 5632].rearrange("p (t k) -> p t k", t=T)
        p2 = V_flat[:, at + 5632:at + 6144].rearrange("p (t k) -> p t k", t=T)
        p2T = V_flat[:, at + 6144:at + 6656].rearrange("p (t k) -> p t k", t=T)
        silu = V_flat[:, at + 6656:at + 7680].rearrange("p (s t) -> p s t", s=2)
        hid = V_flat[:, at:at + 1024].rearrange("p (s t) -> p s t", s=2)

        ps_a = ctx.enter_context(nc.psum_tensor("ps_a", [P, 2, 512], F32))
        ps_b = ctx.enter_context(nc.psum_tensor("ps_b", [P, 2, 1024], F32))
        ps_v = ctx.enter_context(nc.psum_tensor("ps_v", [P, 512], F32))
        ps_m = ctx.enter_context(nc.psum_tensor("ps_m", [P, 512], F32))
        BANK = [ps_a[:, 0, :], ps_a[:, 1, :], ps_b[:, 0, 0:512], ps_b[:, 0, 512:1024],
                ps_b[:, 1, 0:512], ps_b[:, 1, 512:1024], ps_v[:, :], ps_m[:, :]]
        max_rows = ps_m[STACK:STACK + PARTS, 0:Q]
        o_cols = ps_m[:, Q:Q + 64].rearrange("p (t d) -> p t d", t=2)

        x_in, wq_in, wk_in, wv_in, wo_in, small_in = (sem(n) for n in ("x_in", "wq_in", "wk_in", "wv_in", "wo_in", "small_in"))
        mask_q_in, mask_k_in, self_in, out_done = (sem(n) for n in ("mask_q_in", "mask_k_in", "self_in", "out_done"))
        ctx_in_s = [sem(f"ctx_in{j}") for j in range(2)]
        k_out = [[sem(f"k_out{b}{j}") for j in range(2)] for b in range(B)]
        q_out = sem("q_out")
        stack_in = [sem(f"stack_in{j}") for j in range(SLOTS)]
        up_in = [sem(f"up_in{j}") for j in range(2)]
        down_in = [sem(f"down_in{j}") for j in range(2)]
        pool_consts, vh_set, consts, ones_set, dve_own = (sem(n) for n in ("pool_consts", "vh_set", "consts", "ones_set", "dve_own"))
        var_ready, rstd_ready, xn_ready, xnT_ps, xnT_ready = (sem(n) for n in ("var_ready", "rstd_ready", "xn_ready", "xnT_ps", "xnT_ready"))
        masks_ready = sem("masks_ready")
        k_ps, kh_ready, km_ready, v_ps = (sem(n) for n in ("k_ps", "kh_ready", "km_ready", "v_ps"))
        w_high_ready, w_split, ctx_high_ready, ctx_split = (sem(n) for n in ("w_high_ready", "w_split", "ctx_high_ready", "ctx_split"))
        k_rest = sem("k_rest")
        kl_ready = [sem(f"kl_ready{e}") for e in range(2)]
        v_stored = [sem(f"v_stored{j}") for j in range(2)]
        q_ps, q_high, q_split = sem("q_ps"), sem("q_high"), sem("q_split")
        a_ps, tiles_seen, a_max, chain, neg_ready, rows_ps, rows_ready = (sem(n) for n in ("a_ps", "tiles_seen", "a_max", "chain", "neg_ready", "rows_ps", "rows_ready"))
        b_ps, exp_done, pool_masked, dve_masked, pv_done, vh_ready = (sem(n) for n in ("b_ps", "exp_done", "pool_masked", "dve_masked", "pv_done", "vh_ready"))
        oT_ready, o_ps, o_stored = sem("oT_ready"), sem("o_ps"), sem("o_stored")
        attn_ready, aT_ps, aT_ready, wo_ps = (sem(n) for n in ("attn_ready", "aT_ps", "aT_ready", "wo_ps"))
        qk2_ps, qk2_ready, v2_ps, v2_ready = (sem(n) for n in ("qk2_ps", "qk2_ready", "v2_ps", "v2_ready"))
        s2_ps, s2_ready, p2_ready, p2T_ps, p2T_ready, o2_ps = (sem(n) for n in ("s2_ps", "s2_ready", "p2_ready", "p2T_ps", "p2T_ready", "o2_ps"))
        gate_ps, gate_sub, gate_exp = sem("gate_ps"), sem("gate_sub"), sem("gate_exp")
        xnT_high_ready, xnT_split = sem("xnT_high_ready"), sem("xnT_split")
        up_high_ready, up_split, down_high_ready, down_split = (sem(n) for n in ("up_high_ready", "up_split", "down_high_ready", "down_split"))
        up_ps, silu_ready, hid_ready, hid_high_ready, hid_split, down_ps, summed = (sem(n) for n in (
            "up_ps", "silu_ready", "hid_ready", "hid_high_ready", "hid_split", "down_ps", "summed"))

        block = ctx.enter_context(nc.Block())

        def all_chunks(eng, chunk, after_first, after_q, before_last=lambda: None):
            with eng.Fori(0, NC // 2) as i:
                for c in range(2):
                    chunk(c, i)
            after_first()
            for c in range(NC, NC + 2):
                chunk(c, 0)
            after_q()
            with eng.Fori(0, NC // 2 - 2) as i:
                for c in range(NC + 2, NC + 4):
                    chunk(c, i)
            before_last()
            for c in range(2 * NC - 2, 2 * NC):
                chunk(c, 0)

        FIRST, LAST = UNITS, STEPS - 3 * UNITS

        @block.sync
        def _(sp):
            for b in range(B):
                for j in range(2):
                    sp.sem_inc(k_out[b][j], 1)
            sp.dma_start(w_raw[:, 0], wk).then_inc(wk_in, 16)
            sp.dma_start(ctx_raw[:, 0], ctx_in[0]).then_inc(ctx_in_s[0], 16)
            sp.dma_start(w_raw[:, 1], wv).then_inc(wv_in, 16)
            sp.dma_start(ctx_raw[:, 1], ctx_in[1]).then_inc(ctx_in_s[1], 16)
            sp.dma_start(xs[:], x.rearrange("(t p) e -> p t e", p=P)).then_inc(x_in, 16)
            sp.dma_start(raw_k, mask_k.rearrange("(t p) q -> p t q", p=P)).then_inc(mask_k_in, 16)
            sp.dma_start(raw_q, mask_q.rearrange("(t p) k -> p t k", p=P)).then_inc(mask_q_in, 16)
            sp.dma_start(w_q[:], wq).then_inc(wq_in, 16)
            sp.dma_start(w_o[:], wo).then_inc(wo_in, 16)
            sp.dma_start(bias_qk[:, 0, :], bq).then_inc(small_in, 16)
            sp.dma_start(bias_qk[:, 1, :], bk).then_inc(small_in, 16)
            sp.dma_start(bias_v[:], bv.rearrange("(o e) -> o e", o=1)).then_inc(small_in, 16)
            sp.dma_start(w_g[:], gate_w.rearrange("(a p) n -> p a n", p=P)).then_inc(small_in, 16)

            def serve_chunk(c, i):
                b, j = c // NC, c % 2
                if c < 2 * NC - 2:
                    sp.wait_ge(ctx_split, i * 2 + (c + 1))
                    sp.dma_start(ctx_raw[:, j], ctx_in[i * 2 + (c + 2)]).then_inc(ctx_in_s[j], 16)
                for e in range(2):
                    sp.wait_ge(kl_ready[e], i * 2 + (c + 2))
                    rows = k_parts[:, b * H + e * 8:b * H + e * 8 + 8].rearrange("a h d k -> (h d) a k")
                    sp.dma_start(rows[:, :, bass.ds(i * (2 * CK) + (c % NC) * CK, CK)], kp[:, j, e]).then_inc(k_out[b][j], 16)

            def load_stacks(n, slot):
                sp.dma_start(kst[slot][0:48, :], k_parts[0:3, n]).then_inc(stack_in[slot], 16)
                sp.dma_start(kst[slot][48:80, :], k_parts[0:2, n]).then_inc(stack_in[slot], 16)
                sp.dma_start(kst[slot][80:96, :], k_parts[0, n]).then_inc(stack_in[slot], 16)
                sp.dma_start(qst[0:48, slot, :], q_parts[0:1, n].broadcast_to([3, D, Q])).then_inc(stack_in[slot], 16)
                sp.dma_start(qst[48:80, slot, :], q_parts[1:2, n].broadcast_to([2, D, Q])).then_inc(stack_in[slot], 16)
                sp.dma_start(qst[80:96, slot, :], q_parts[2, n]).then_inc(stack_in[slot], 16)

            def serve_q():
                for e in range(KIN):
                    sp.wait_ge(q_split, e + 1)
                    for a in range(PARTS):
                        to = q_parts[a].rearrange("(b h) d q -> (h d) b q", b=B)[e * P:(e + 1) * P]
                        sp.dma_start(to, qp[:, a, e, :].rearrange("p (b q) -> p b q", b=B)).then_inc(q_out, 16)

            def load_first():
                sp.wait_ge(q_out, 16 * PARTS * KIN)
                for j in range(2):
                    sp.wait_ge(k_out[0][j], 16 * NC + 1)
                for n in range(2):
                    load_stacks(n, n)

            all_chunks(sp, serve_chunk, lambda: None, serve_q, load_first)
            sp.wait_ge(v_ps, 2 * B * NC)
            for j in range(2):
                sp.wait_ge(k_out[1][j], 16 * NC + 1)
            for n in range(2, SLOTS):
                load_stacks(n, n)
            with sp.Fori(0, NH // SLOTS - 1) as i:
                for slot in range(SLOTS):
                    n = sp.snap(i * SLOTS + (SLOTS + slot))
                    sp.wait_ge(b_ps, i * (SLOTS * UNITS) + (slot + 1) * UNITS)
                    load_stacks(n, slot)

            def load_up(e, s):
                sp.dma_start(up_sb[:, s], up_w[e]).then_inc(up_in[s], 16)

            def load_down(e, s):
                sp.dma_start(down_sb[:, s], down_w[e].rearrange("(a p) n -> p a n", p=P)).then_inc(down_in[s], 16)

            sp.wait_ge(vh_ready, H)
            for e in range(2):
                load_up(e, e)
                load_down(e, e)
            for m, w in enumerate((sq, sk, sv)):
                sp.dma_start(self_w[:, m], w).then_inc(self_in, 16)
            with sp.Fori(0, NE // 2 - 1) as i:
                for s in range(2):
                    e = sp.snap(i * 2 + (s + 2))
                    sp.wait_ge(up_split, i * 2 + (s + 1))
                    load_up(e, s)
                    sp.wait_ge(down_split, i * 2 + (s + 1))
                    load_down(e, s)
            sp.wait_ge(summed, NE * T + 1)
            sp.dma_start(out.rearrange("(t p) e -> p t e", p=P), xs[:]).then_inc(out_done, 16)
            sp.wait_ge(out_done, 16)

        @block.gpsimd
        def _(pool):
            for e in range(2):
                pool.sem_inc(kl_ready[e], 1)
            pool.memset(neg_half[:], -0.5).then_inc(pool_consts, 1)
            pool.memset(ident[:], 0.0).then_inc(pool_consts, 1)
            pool.memset(fold[:], 0.0).then_inc(pool_consts, 1)
            pool.memset(group_bias[:], 0.0).then_inc(pool_consts, 1)
            pool.wait_ge(pool_consts, 4)
            pool.affine_select(out=ident[:], in_=ident[:], compare_op=ALU.not_equal, fill=1.0, base=0,
                               pattern=[[-1, P]], channel_multiplier=1).then_inc(consts, 1)

            def rstds(n):
                pool.wait_ge(var_ready, n + 1)
                pool.tensor_tensor(rstd[:], var_eps[:], neg_half[:], ALU.pow).then_inc(rstd_ready, 1)

            rstds(0)
            for g in range(4):
                pool.affine_select(out=fold[:], in_=fold[:], compare_op=ALU.not_equal, fill=1.0, base=-32 * g,
                                   pattern=[[-1, 32]], channel_multiplier=1).then_inc(pool_consts, 1)
                pool.wait_ge(pool_consts, 5 + g)
            pool.affine_select(out=group_bias[:], in_=group_bias[:], compare_op=ALU.is_ge, fill=-BIG, base=0,
                               pattern=[[-GROUP, P // GROUP], [0, GROUP]], channel_multiplier=1).then_inc(pool_consts, 1)
            pool.wait_ge(pool_consts, 9)
            pool.affine_select(out=group_bias[:], in_=group_bias[:], compare_op=ALU.is_ge, fill=-BIG, base=GROUP - 1,
                               pattern=[[GROUP, P // GROUP], [0, GROUP]], channel_multiplier=-1).then_inc(consts, 1)
            pool.wait_ge(consts, 3)
            pool.memset(kst_early[STACK:ROWS, :, :], 1.0).then_inc(ones_set, 1)
            pool.wait_ge(ones_set, 1)

            with pool.Fori(0, B * NC // 2) as i:
                for j in range(2):
                    for e in range(2):
                        pool.wait_ge(km_ready, i * 4 + (2 * j + e + 1))
                        pool.tensor_tensor(kp[:, j, e, 2, :], rest[:, e, :], kp[:, j, e, 1, :],
                                           ALU.subtract).then_inc(kl_ready[e], 1)
            pool.wait_ge(v_ps, 2 * B * NC)
            for e in range(2):
                pool.wait_ge(kl_ready[e], B * NC + 1)
            pool.memset(Vh[:], 0.0).then_inc(vh_set, 1)
            pool.wait_ge(vh_set, 1)
            pool.memset(Vh[:, :, :, D:D + 1], 1.0).then_inc(vh_set, 1)
            pool.wait_ge(vh_set, 2)
            pool.memset(kst_late[STACK:ROWS, :, :], 1.0).then_inc(ones_set, 1)
            pool.wait_ge(ones_set, 2)

            pool.wait_ge(masks_ready, 2 * NC + 1)
            with pool.Fori(0, NH) as n:
                for u in range(UNITS):
                    if u in POOL_UNITS:
                        pool.wait_ge(exp_done, n * UNITS + (u + 1))
                        tile = probs[:, u % 4, :]
                        keep = mask_int[:, INT_UNITS.index(u)].rearrange("p k q -> p (k q)")
                        pool.tensor_tensor(tile.bitcast(I32), tile.bitcast(I32), keep, ALU.mult).then_inc(pool_masked, 1)
            rstds(1)

            def low_weights(base, e):
                s = e % 2
                pool.wait_ge(up_high_ready, base + (e + 1))
                pool.tensor_tensor(up_low[:, s], up_sb[:, s], up_high[:, s].bitcast(F32), ALU.subtract).then_inc(up_split, 1)
                pool.wait_ge(down_high_ready, base + (e + 1))
                pool.tensor_tensor(down_low[:, s], down_sb[:, s], down_high[:, s].bitcast(F32),
                                   ALU.subtract).then_inc(down_split, 1)

            low_weights(0, 0)
            rstds(2)
            low_weights(0, 1)
            with pool.Fori(0, NE // 2 - 1) as i:
                for j in range(2):
                    low_weights(i * 2, j + 2)

        @block.scalar
        def _(act):
            act.wait_ge(consts, 1)
            act.activation(ident_bf[:], ident[:], ACT.Copy).then_inc(consts, 1)

            def high_chunk(c, i):
                j = c % 2
                act.wait_ge(ctx_in_s[j], i * 16 + 16 * (c // 2 + 1))
                act.activation(ctx_high[:, j], ctx_raw[:, j], ACT.Copy).then_inc(ctx_high_ready, 1)

            def split_k(c, i):
                b, j = c // NC, c % 2
                if c in (NC, NC + 1):
                    act.wait_ge(k_out[0][j], 16 * NC + 1)
                else:
                    act.wait_ge(k_out[b][j], i * 32 + (32 * (c % NC // 2) + 1))
                for e in range(2):
                    act.wait_ge(k_ps, i * 4 + (2 * c + e + 1))
                    act.activation(kp[:, j, e, 0, :], BANK[e], ACT.Copy).then_inc(kh_ready, 1)
                for e in range(2):
                    act.wait_ge(k_rest, i * 4 + (2 * c + e + 2))
                    act.activation(kp[:, j, e, 1, :], rest[:, e, :], ACT.Copy).then_inc(km_ready, 1)
                if b == 0:
                    part = bass.ds(i * (2 * MASK_SLICE) + c * MASK_SLICE, MASK_SLICE)
                    act.activation(mask_int_flat[:, part], raw_k_flat[:, bass.ds(
                        i * (2 * MASK_SLICE) + (c * MASK_SLICE + len(PE_UNITS) * UT * Q), MASK_SLICE)],
                        ACT.Copy).then_inc(masks_ready, 1)
                if c < 2 * NC - 2:
                    act.wait_ge(v_ps, i * 4 + 2 * (c + 1))
                    high_chunk(c + 2, i)

            for w, arrived in enumerate((wk_in, wv_in)):
                act.wait_ge(arrived, 16)
                act.activation(w_high[:, w], w_raw[:, w], ACT.Copy).then_inc(w_high_ready, 1)
                high_chunk(w, 0)
            act.wait_ge(mask_k_in, 16)

            def turn_x():
                for k in range(T // 2):
                    act.wait_ge(xnT_ps, 2 * (k + 1))
                    act.activation(xnT[:, :, k * 2 * P:(k + 1) * 2 * P].rearrange("p a (t q) -> p t a q", t=2),
                                   BANK[6 + k].rearrange("p (t a q) -> p t a q", t=2, a=KIN), ACT.Copy).then_inc(xnT_ready, 2)

            def high_q():
                for e in range(KIN):
                    act.wait_ge(q_ps, e + 1)
                    act.activation(qp[:, 0, e, :], BANK[6 + e], ACT.Copy, scale=float(D) ** -0.5).then_inc(q_high, 1)

            all_chunks(act, split_k, turn_x, high_q)

            def copy_xnT(n, first_bank):
                for t in range(T):
                    act.wait_ge(xnT_ps, T * n + t + 1)
                    act.activation(xnT[:, :, t * P:(t + 1) * P],
                                   BANK[first_bank + t][:, 0:E].rearrange("p (a q) -> p a q", a=KIN),
                                   ACT.Copy).then_inc(xnT_ready, 1)

            def copy_vh(n, p):
                act.activation(Vh[:, p, :, 0:D], V[:, n], ACT.Copy).then_inc(vh_ready, 1)

            def exp_unit(base, g):
                act.wait_ge(b_ps, base + g + 1)
                if g >= 4:
                    act.wait_ge(pv_done, base + (g - 3))
                act.activation(probs[:, g % 4, :], ps_b[:, g % 2, :], ACT.Exp).then_inc(exp_done, 1)

            def copy_rows(base, n):
                act.wait_ge(rows_ps, base + n + 1)
                act.activation(qst[STACK:ROWS, n % SLOTS, :], max_rows, ACT.Copy).then_inc(rows_ready, 1)

            def copy_oT(base, n):
                act.wait_ge(pv_done, base * UNITS + UNITS * (n + 1))
                if n >= 2:
                    act.wait_ge(o_ps, base + (n - 1))
                act.activation(oT[:, n % 2, :], ps_v[:, 0:Q], ACT.Copy).then_inc(oT_ready, 1)

            for b in range(2):
                act.wait_ge(v_stored[b], 2 * NC + 1)
            for e in range(2):
                act.wait_ge(kl_ready[e], B * NC + 1)
            copy_rows(0, 0)
            for g in range(LEAD_B):
                exp_unit(0, g)
            act.wait_ge(vh_set, 2)
            copy_vh(0, 0)

            def step(base, heads, s):
                if s % UNITS == 0 and s > 0:
                    copy_oT(heads, s // UNITS - 1)
                if s % UNITS == 4 and s // UNITS + 1 < NH:
                    copy_rows(heads, s // UNITS + 1)
                if s + LEAD_B < STEPS:
                    exp_unit(base, s + LEAD_B)
                if s % UNITS == 6 and s // UNITS + 1 < NH:
                    n = s // UNITS + 1
                    if n >= 2:
                        act.wait_ge(pv_done, base + UNITS * (n - 1))
                    copy_vh(heads + n, n % 2)

            for s in range(FIRST):
                step(0, 0, s)
            body = SLOTS * UNITS
            with act.Fori(0, (LAST - FIRST) // body) as i:
                for s in range(FIRST, FIRST + body):
                    step(i * body, i * SLOTS, s)
            for s in range(LAST, STEPS):
                step(0, 0, s)
            copy_oT(0, NH - 1)

            def high_up(base, e):
                s = e % 2
                act.wait_ge(up_in[s], base * 8 + 16 * (e // 2 + 1))
                if e >= 2:
                    act.wait_ge(up_ps, base * FT + FT * (e - 1))
                act.activation(up_high[:, s], up_sb[:, s], ACT.Copy).then_inc(up_high_ready, 1)

            def high_down(base, e):
                s = e % 2
                act.wait_ge(down_in[s], base * 8 + 16 * (e // 2 + 1))
                if e >= 2:
                    act.wait_ge(down_ps, base * T + T * (e - 1))
                act.activation(down_high[:, s], down_sb[:, s], ACT.Copy).then_inc(down_high_ready, 1)

            for t in range(T):
                act.wait_ge(aT_ps, t + 1)
                act.activation(aT[:, t, :], BANK[t][:, 0:E], ACT.Copy).then_inc(aT_ready, 1)
            high_up(0, 0)
            high_down(0, 0)
            copy_xnT(1, 0)
            act.wait_ge(small_in, 64)
            for m, to in enumerate((q2T, k2T)):
                for e in range(KIN):
                    act.wait_ge(qk2_ps, 2 * m + e + 1)
                    act.activation(to[:, e, :], BANK[4 + 2 * m + e], ACT.Identity,
                                   bias=bias_qk[:, m, e:e + 1]).then_inc(qk2_ready, 1)
            for t in range(T):
                act.wait_ge(s2_ready, t + 1)
                act.activation(p2[:, t, :], s2[:, t, :], ACT.Exp, bias=tk[:, 1, t:t + 1],
                               accum_out=tk[:, 2, t:t + 1]).then_inc(p2_ready, 1)
            for t in range(T):
                act.wait_ge(p2T_ps, t + 1)
                act.activation(p2T[:, t, :], BANK[t][:, 256:384], ACT.Copy).then_inc(p2T_ready, 1)
            high_up(0, 1)
            high_down(0, 1)
            copy_xnT(2, 0)
            act.wait_ge(gate_sub, 1)
            act.activation(lg[:, 1], lg[:, 0], ACT.Exp).then_inc(gate_exp, 1)

            for t in range(T):
                act.wait_ge(xnT_ready, 2 * T + t + 1)
            act.activation(xnT_high[:], xnT[:], ACT.Copy).then_inc(xnT_high_ready, 1)

            def gates(base, e):
                for f in range(FT):
                    act.wait_ge(up_ps, base * FT + (FT * e + f + 1))
                    act.activation(silu[:, f % 2, :], BANK[2 * (f % 2)], ACT.Silu).then_inc(silu_ready, 1)
                    act.wait_ge(hid_ready, base * FT + (FT * e + f + 1))
                    act.activation(hid_high[:, e % 2, f, :], hid[:, f % 2, :], ACT.Copy).then_inc(hid_high_ready, 1)

            gates(0, 0)
            with act.Fori(0, NE // 2 - 1) as i:
                for j in range(2):
                    high_up(i * 2, j + 2)
                    gates(i * 2, j + 1)
                    high_down(i * 2, j + 2)
            gates(0, NE - 1)

        @block.vector
        def _(dve):
            count = [0]

            def link(ins):
                count[0] += 1
                ins.then_inc(dve_own, 1)
                dve.wait_ge(dve_own, count[0])

            def mark(ins):
                count[0] += 1
                ins.then_inc(dve_own, 1)

            def layer_norm(n):
                for t in range(T):
                    mark(dve.bn_stats(stats[:, t, :], xs[:, t, :]))
                dve.wait_ge(dve_own, count[0])
                for t in range(T):
                    mark(dve.bn_aggr(mean_var[:, t, :], stats[:, t, :]))
                dve.wait_ge(dve_own, count[0])
                dve.tensor_scalar(var_eps[:], mean_var[:, :, 1], EPS, None, ALU.add).then_inc(var_ready, 1)
                dve.wait_ge(rstd_ready, n + 1)
                for t in range(T):
                    dve.tensor_scalar(xn[:, t, :], xs[:, t, :], mean_var[:, t, 0:1], rstd[:, t:t + 1],
                                      ALU.subtract, ALU.mult).then_inc(xn_ready, 1)

            for j in range(2):
                dve.sem_inc(v_stored[j], 1)
            dve.sem_inc(k_rest, 1)
            dve.sem_inc(summed, 1)
            def low_chunk(c, i):
                dve.wait_ge(ctx_high_ready, i * 2 + (c + 1))
                dve.tensor_tensor(ctx_low[:, c % 2], ctx_raw[:, c % 2], ctx_high[:, c % 2].bitcast(F32),
                                  ALU.subtract).then_inc(ctx_split, 1)

            def store_kv(c, i):
                b, j = c // NC, c % 2
                for e in range(2):
                    dve.wait_ge(kh_ready, i * 4 + (2 * c + e + 1))
                    dve.wait_ge(kl_ready[e], i * 2 + (c + 1))
                    dve.tensor_tensor(rest[:, e, :], BANK[e], kp[:, j, e, 0, :],
                                      ALU.subtract).then_inc(k_rest, 1)
                for v in range(2):
                    dve.wait_ge(v_ps, i * 4 + (2 * c + v + 1))
                    to = V[:, b * H:(b + 1) * H, bass.ds(i * 8 + (4 * (c % NC) + 2 * v), 2), :]
                    dve.tensor_copy(to, BANK[2 + 2 * j + v].rearrange("p (k h d) -> p h k d", k=2, h=H)
                                    ).then_inc(v_stored[j], 1)
                if c < 2 * NC - 2:
                    low_chunk(c + 2, i)
                if b == 0:
                    keys = bass.ds(i * (2 * CK) + c * CK, CK)
                    dve.tensor_scalar(mask_bias[:, :, keys], raw_q[:, :, keys], BIG, -BIG, ALU.mult,
                                      ALU.add).then_inc(masks_ready, 1)

            for w in range(2):
                dve.wait_ge(w_high_ready, w + 1)
                dve.tensor_tensor(w_low[:, w], w_raw[:, w], w_high[:, w].bitcast(F32), ALU.subtract).then_inc(w_split, 1)
                low_chunk(w, 0)
            dve.wait_ge(x_in, 16)
            layer_norm(0)
            dve.wait_ge(mask_k_in, 16)
            for u in PE_UNITS:
                ins = dve.tensor_scalar(mask_turned[:, PE_UNITS.index(u)], raw_k[:, PE_UNITS.index(u) * UT:(PE_UNITS.index(u) + 1) * UT, :], BIG, -BIG,
                                        ALU.mult, ALU.add)
            ins.then_inc(masks_ready, 1)
            dve.wait_ge(mask_q_in, 16)

            def split_q():
                for e in range(KIN):
                    dve.wait_ge(q_high, e + 1)
                    rest_q = xn[:, 2 * e:2 * e + 2, :].rearrange("p t e -> p (t e)")
                    link(dve.scalar_tensor_tensor(rest_q, BANK[6 + e], float(D) ** -0.5, qp[:, 0, e, :],
                                                  ALU.mult, ALU.subtract))
                    link(dve.tensor_copy(qp[:, 1, e, :], rest_q))
                    dve.tensor_tensor(qp[:, 2, e, :], rest_q, qp[:, 1, e, :], ALU.subtract).then_inc(q_split, 1)

            all_chunks(dve, store_kv, lambda: dve.wait_ge(masks_ready, 2 * NC + 1), split_q)
            for n in range(NE):
                ins = dve.memset(rank[:, n:n + 1], float(NE - n))
            mark(ins)
            mark(dve.memset(ones_row[:], 1.0))
            def maxima(base, a, t):
                u, n = a % UNITS, a // UNITS
                dve.wait_ge(a_ps, base * 2 + (2 * a + t + 1))
                dve.sem_inc(tiles_seen, 1)
                dve.tensor_tensor_reduce(unused[:, t, :], ps_a[:, t, :], mask_bias[:, t, u * UK:(u + 1) * UK],
                                         1.0, -BIG, ALU.add, ALU.max,
                                         unit_max[:, n % 2, t, u:u + 1]).then_inc(a_max, 1)

            def negate_max(heads, n, part):
                p = n % 2
                if part == 0:
                    dve.wait_ge(a_max, heads * 16 + 16 * (n + 1))
                    dve.tensor_reduce(head_max[:, p, :], unit_max[:, p], AX, ALU.max).then_inc(chain, 1)
                    return
                dve.wait_ge(chain, heads * 4 + (4 * n + part))
                if part == 1:
                    dve.tensor_scalar(any_kept[:, heads + n, :], head_max[:, p, :], -1e38, None, ALU.is_gt)
                    dve.tensor_scalar(neg_parts[:, p, :, 0], head_max[:, p, :], -1.0, None, ALU.mult).then_inc(chain, 1)
                elif part == 2:
                    dve.scalar_tensor_tensor(neg_rest[:, p, :], head_max[:, p, :], -1.0, neg_parts[:, p, :, 0],
                                             ALU.mult, ALU.subtract).then_inc(chain, 1)
                elif part == 3:
                    dve.tensor_copy(neg_parts[:, p, :, 1], neg_rest[:, p, :]).then_inc(chain, 1)
                else:
                    dve.tensor_tensor(neg_parts[:, p, :, 2], neg_rest[:, p, :], neg_parts[:, p, :, 1],
                                      ALU.subtract).then_inc(neg_ready, 1)

            def mask_unit(base, g, part):
                keep = mask_int[:, INT_UNITS.index(g % UNITS)].rearrange("p k q -> p (k q)")
                cols = slice(part * UT * Q // 2, (part + 1) * UT * Q // 2)
                if part == 0:
                    dve.wait_ge(exp_done, base + g + 1)
                dve.scalar_tensor_tensor(probs[:, g % 4, cols], probs[:, g % 4, cols], BIG, keep[:, cols], ALU.min,
                                         ALU.mult).then_inc(dve_masked, 1)

            def store_o(heads, n):
                dve.wait_ge(o_ps, heads + n + 1)
                dve.tensor_copy(O[:, heads + n, :, :], o_cols[:, :, 0:D + 1]).then_inc(o_stored, 1)

            for a in range(LEAD_A):
                if a == UNITS:
                    for part in range(5):
                        negate_max(0, 0, part)
                for t in range(2):
                    maxima(0, a, t)

            def step(base, heads, s):
                for t in range(2):
                    if s + LEAD_A < STEPS:
                        maxima(base, s + LEAD_A, t)
                    part = 2 * (s % UNITS) + t - 3
                    if 0 <= part < 5 and s // UNITS + 1 < NH:
                        negate_max(heads, s // UNITS + 1, part)
                    g = s + 1 + t
                    if g < STEPS and g % UNITS in DVE_UNITS:
                        mask_unit(base, g, 1 - t)
                if s % UNITS == 2 and s >= UNITS:
                    store_o(heads, s // UNITS - 1)

            for s in range(FIRST):
                step(0, 0, s)
            with dve.Fori(0, (LAST - FIRST) // (2 * UNITS)) as i:
                for s in range(FIRST, FIRST + 2 * UNITS):
                    step(i * (2 * UNITS), i * 2, s)
            for s in range(LAST, STEPS):
                step(0, 0, s)
            store_o(0, NH - 1)
            dve.wait_ge(o_stored, NH)

            link(dve.tensor_tensor(norm[:], O[:, :, :, D], any_kept[:], ALU.mult))
            link(dve.reciprocal(norm[:], norm[:]))
            link(dve.tensor_tensor(norm[:], norm[:], any_kept[:], ALU.mult))
            for b in range(B):
                for t in range(2):
                    dve.tensor_tensor(attn[:, 2 * b + t, :].rearrange("p (h d) -> p h d", h=H),
                                      O[:, b * H:(b + 1) * H, t, 0:D],
                                      norm[:, b * H:(b + 1) * H, t:t + 1].broadcast_to([P, H, D]),
                                      ALU.mult).then_inc(attn_ready, 1)
            for t in range(T):
                dve.wait_ge(wo_ps, t + 1)
                mark(dve.tensor_tensor(xs[:, t, :], xs[:, t, :], BANK[4 + t][:, 0:E], ALU.add))
            dve.wait_ge(dve_own, count[0])
            layer_norm(1)
            for t in range(T):
                dve.wait_ge(v2_ps, t + 1)
                dve.tensor_copy(v2[:, t, :], BANK[t][:, 0:E]).then_inc(v2_ready, 1)
            group_b = group_bias[:].rearrange("p a b -> p (a b)")
            dve.wait_ge(consts, 3)
            for t in range(T):
                dve.wait_ge(s2_ps, t + 1)
                link(dve.tensor_tensor_reduce(s2[:, t, :], BANK[4 + t][:, 0:P], group_b, 1.0, -BIG,
                                              ALU.add, ALU.max, tk[:, 0, t:t + 1]))
                dve.tensor_scalar(tk[:, 1, t:t + 1], tk[:, 0, t:t + 1], -1.0, None, ALU.mult).then_inc(s2_ready, 1)
            dve.wait_ge(p2_ready, T)
            link(dve.reciprocal(tk[:, 3, :], tk[:, 2, :]))
            for t in range(T):
                dve.wait_ge(o2_ps, t + 1)
                mark(dve.scalar_tensor_tensor(xs[:, t, :], BANK[4 + t][:, 256:512], tk[:, 3, t:t + 1], xs[:, t, :],
                                              ALU.mult, ALU.add))
            dve.wait_ge(dve_own, count[0])
            layer_norm(2)

            def wide(col):
                return col.rearrange("p (t o) -> p t o", o=1).broadcast_to([P, T, NE])

            ranks = rank[:].rearrange("p (o n) -> p o n", o=1).broadcast_to([P, T, NE])
            logits = ps_m[:, 0:T * NE].rearrange("p (t n) -> p t n", t=T)
            dve.wait_ge(gate_ps, 1)
            link(dve.tensor_reduce(tk[:, 4, :], logits, AX, ALU.max))
            dve.tensor_tensor(lg[:, 0], logits, wide(tk[:, 4, :]), ALU.subtract).then_inc(gate_sub, 1)
            dve.wait_ge(gate_exp, 1)
            link(dve.tensor_reduce(tk[:, 5, :], lg[:, 1], AX, ALU.add))
            link(dve.reciprocal(tk[:, 5, :], tk[:, 5, :]))
            link(dve.tensor_tensor(lg[:, 2], lg[:, 1], wide(tk[:, 5, :]), ALU.mult))

            def pick(values, best, chosen):
                link(dve.tensor_reduce(tk[:, best, :], values, AX, ALU.max))
                link(dve.tensor_tensor(lg[:, 3], values, wide(tk[:, best, :]), ALU.is_equal))
                link(dve.tensor_tensor(lg[:, 3], lg[:, 3], ranks, ALU.mult))
                link(dve.tensor_reduce(tk[:, 4, :], lg[:, 3], AX, ALU.max))
                link(dve.tensor_tensor(chosen, lg[:, 3], wide(tk[:, 4, :]), ALU.is_equal))

            pick(lg[:, 2], 6, lg[:, 4])
            link(dve.scalar_tensor_tensor(lg[:, 5], lg[:, 4], -2.0, lg[:, 2], ALU.mult, ALU.add))
            pick(lg[:, 5], 7, lg[:, 6])
            link(dve.tensor_tensor(tk[:, 5, :], tk[:, 6, :], tk[:, 7, :], ALU.add))
            link(dve.reciprocal(tk[:, 5, :], tk[:, 5, :]))
            link(dve.tensor_tensor(lg[:, 4], lg[:, 4], lg[:, 6], ALU.add))
            link(dve.tensor_tensor(lg[:, 4], lg[:, 4], lg[:, 2], ALU.mult))
            link(dve.tensor_tensor(wgt[:].rearrange("p n t -> p t n"), lg[:, 4], wide(tk[:, 5, :]), ALU.mult))

            def hidden(base, e):
                for f in range(FT):
                    dve.wait_ge(silu_ready, base * FT + (FT * e + f + 1))
                    dve.tensor_tensor(hid[:, f % 2, :], silu[:, f % 2, :], BANK[2 * (f % 2) + 1],
                                      ALU.mult).then_inc(hid_ready, 1)
                    dve.wait_ge(hid_high_ready, base * FT + (FT * e + f + 1))
                    dve.tensor_tensor(hid_low[:, e % 2, f, :], hid[:, f % 2, :], hid_high[:, e % 2, f, :].bitcast(F32),
                                      ALU.subtract).then_inc(hid_split, 1)

            def add_expert(base, e):
                for t in range(T):
                    dve.wait_ge(down_ps, base * T + (T * e + t + 1))
                    dve.scalar_tensor_tensor(xs[:, t, :], BANK[4 + t][:, 0:E], wgt[:, base + e, t:t + 1],
                                             xs[:, t, :], ALU.mult, ALU.add).then_inc(summed, 1)

            dve.wait_ge(xnT_high_ready, 1)
            dve.tensor_tensor(xnT_low[:], xnT[:], xnT_high[:].bitcast(F32), ALU.subtract).then_inc(xnT_split, 1)
            hidden(0, 0)
            with dve.Fori(0, NE // 2 - 1) as i:
                for j in range(2):
                    hidden(i * 2, j + 1)
                    add_expert(i * 2, j)
            hidden(0, NE - 1)
            add_expert(0, NE - 2)
            add_expert(0, NE - 1)

        @block.tensor
        def _(pe):
            def transpose_xn(n, first_bank):
                for t in range(T):
                    pe.wait_ge(xn_ready, T * n + t + 1)
                    for a in range(KIN):
                        ins = pe.transpose(BANK[first_bank + t][:, a * P:(a + 1) * P], xn[:, t, a * P:(a + 1) * P],
                                           ident[:])
                    ins.then_inc(xnT_ps, 1)

            def product(out, high, low, to_high, to_low, start, stop):
                pe.matmul(out, high, to_high, start=start, stop=False)
                pe.matmul(out, high, to_low, start=False, stop=False)
                return pe.matmul(out, low, to_high, start=False, stop=stop)

            def project_kv(c, i):
                j = c % 2
                pe.wait_ge(ctx_split, i * 2 + (c + 1))
                pe.wait_ge(k_rest, i * 4 + (2 * c + 1))
                for e in range(2):
                    for a in range(KIN):
                        cols = slice(e * P, (e + 1) * P)
                        ins = product(BANK[e], w_high[:, 0, a, cols], w_low[:, 0, a, cols],
                                      ctx_high[:, j, a, :], ctx_low[:, j, a, :], a == 0, a == KIN - 1)
                    ins.then_inc(k_ps, 1)
                pe.wait_ge(v_stored[j], i * 2 + (2 * (c // 2) + 1))
                for v in range(2):
                    for k in range(2):
                        for a in range(KIN):
                            keys = slice((2 * v + k) * P, (2 * v + k + 1) * P)
                            ins = product(BANK[2 + 2 * j + v][:, k * E:(k + 1) * E],
                                          ctx_high[:, j, a, keys], ctx_low[:, j, a, keys],
                                          w_high[:, 1, a, :], w_low[:, 1, a, :], a == 0, a == KIN - 1)
                    ins.then_inc(v_ps, 1)

            def turn_x():
                for t in range(T):
                    pe.wait_ge(xn_ready, t + 1)
                    for a in range(KIN):
                        at = ((t % 2) * KIN + a) * P
                        ins = pe.transpose(BANK[6 + t // 2][:, at:at + P], xn[:, t, a * P:(a + 1) * P], ident[:])
                    ins.then_inc(xnT_ps, 1)

            def project_q():
                pe.wait_ge(wq_in, 16)
                pe.wait_ge(xnT_ready, T)
                for e in range(KIN):
                    for a in range(KIN):
                        ins = pe.matmul(BANK[6 + e], w_q[:, a, e * P:(e + 1) * P], xnT[:, a, :],
                                        start=(a == 0), stop=(a == KIN - 1))
                    ins.then_inc(q_ps, 1)

            pe.wait_ge(w_split, 2)
            pe.wait_ge(consts, 1)
            all_chunks(pe, project_kv, turn_x, project_q)

            def scores_for_max(base, a, t):
                n, u = a // UNITS, a % UNITS
                slot = n % SLOTS
                if u == 0 and t == 0:
                    pe.wait_ge(stack_in[slot], base * (16 * LOADS // (SLOTS * UNITS)) + 16 * LOADS * (n // SLOTS + 1))
                if a >= 1:
                    pe.wait_ge(a_max, base * 2 + (2 * a + t - 1))
                pe.matmul(ps_a[:, t, :], qst[0:STACK, slot, t * P:(t + 1) * P],
                          kst[slot][0:STACK, u * UK:(u + 1) * UK], start=True, stop=True).then_inc(a_ps, 1)

            def turn_max(heads, n):
                pe.wait_ge(neg_ready, heads + n + 1)
                if n >= 2:
                    pe.wait_ge(o_stored, heads + (n - 1))
                for t in range(2):
                    ins = pe.matmul(ps_m[STACK:STACK + PARTS, t * P:(t + 1) * P], neg_parts[:, n % 2, t, 0:PARTS],
                                    ident_bf[:], start=True, stop=True)
                ins.then_inc(rows_ps, 1)

            def scores(base, heads, g):
                n, u = g // UNITS, g % UNITS
                slot = n % SLOTS
                if u == 0:
                    pe.wait_ge(rows_ready, heads + n + 1)
                    if slot >= 2:
                        pe.wait_ge(ones_set, 2)
                if g >= 2:
                    pe.wait_ge(exp_done, base + (g - 1))
                if u in PE_UNITS:
                    bias = mask_turned[:, PE_UNITS.index(u)].rearrange("p k q -> p (k q)")
                    for c in range(2):
                        pe.matmul(ps_b[:, g % 2, c * 512:(c + 1) * 512], ident_bf[:],
                                  bias[:, c * 512:(c + 1) * 512], start=True, stop=False, skip_group_check=True)
                for k in range(UT):
                    key = u * UK + k * P
                    ins = pe.matmul(ps_b[:, g % 2, k * Q:(k + 1) * Q], kst[slot][0:ROWS, key:key + P],
                                    qst[0:ROWS, slot, :], start=u not in PE_UNITS, stop=True,
                                    skip_group_check=u in PE_UNITS)
                ins.then_inc(b_ps, 1)

            def values(base, heads, g):
                n, u = g // UNITS, g % UNITS
                if u in POOL_UNITS:
                    masked = n * len(POOL_UNITS) + POOL_UNITS.index(u) + 1
                    pe.wait_ge(pool_masked, heads * len(POOL_UNITS) + masked)
                elif u in DVE_UNITS:
                    masked = n * len(DVE_UNITS) + DVE_UNITS.index(u) + 1
                    pe.wait_ge(dve_masked, heads * 2 * len(DVE_UNITS) + 2 * masked)
                else:
                    pe.wait_ge(exp_done, base + (g + 1))
                if u == 0:
                    pe.wait_ge(vh_ready, heads + n + 1)
                    if n >= 1:
                        pe.wait_ge(oT_ready, heads + n)
                for k in range(UT):
                    ins = pe.matmul(ps_v[32 * k:32 * k + 32, 0:Q], Vh[:, n % 2, u * UT + k, :],
                                    probs[:, g % 4, k * Q:(k + 1) * Q], start=(u == 0), stop=(u == UNITS - 1))
                ins.then_inc(pv_done, 1)

            def fold_o(heads, n):
                pe.wait_ge(oT_ready, heads + n + 1)
                for t in range(2):
                    ins = pe.matmul(o_cols[:, t, 0:D + 1], oT[:, n % 2, t * P:(t + 1) * P], fold[:, 0:D + 1],
                                    start=True, stop=True)
                ins.then_inc(o_ps, 1)

            pe.wait_ge(k_rest, 2 * B * NC + 1)
            for j in range(2):
                pe.wait_ge(v_stored[j], B * NC + 1)
            pe.wait_ge(masks_ready, 2 * NC + 1)
            pe.wait_ge(consts, 3)
            pe.wait_ge(ones_set, 1)
            for a in range(UNITS):
                for t in range(2):
                    scores_for_max(0, a, t)
            turn_max(0, 0)
            for a in range(UNITS, LEAD_A):
                for t in range(2):
                    scores_for_max(0, a, t)
            for g in range(LEAD_B):
                scores(0, 0, g)

            def step(base, heads, s):
                n = s // UNITS
                if s + LEAD_A < STEPS:
                    scores_for_max(base, s + LEAD_A, 0)
                if s % UNITS == 1 and s >= UNITS:
                    fold_o(heads, n - 1)
                if s + LEAD_B < STEPS:
                    scores(base, heads, s + LEAD_B)
                if s % UNITS == 4 and n + 1 < NH:
                    turn_max(heads, n + 1)
                if s + LEAD_A < STEPS:
                    scores_for_max(base, s + LEAD_A, 1)
                values(base, heads, s)

            for s in range(FIRST):
                step(0, 0, s)
            body = SLOTS * UNITS
            with pe.Fori(0, (LAST - FIRST) // body) as i:
                for s in range(FIRST, FIRST + body):
                    step(i * body, i * SLOTS, s)
            for s in range(LAST, STEPS):
                step(0, 0, s)
            pe.wait_ge(o_stored, NH - 1)
            fold_o(0, NH - 1)

            pe.wait_ge(wo_in, 16)
            for t in range(T):
                pe.wait_ge(attn_ready, t + 1)
                for a in range(KIN):
                    ins = pe.transpose(BANK[t][:, a * P:(a + 1) * P], attn[:, t, a * P:(a + 1) * P], ident[:])
                ins.then_inc(aT_ps, 1)
            for t in range(T):
                pe.wait_ge(aT_ready, t + 1)
                for a in range(KIN):
                    ins = pe.matmul(BANK[4 + t][:, 0:E], aT[:, t, a * P:(a + 1) * P], w_o[:, a, :],
                                    start=(a == 0), stop=(a == KIN - 1))
                ins.then_inc(wo_ps, 1)
            transpose_xn(1, 0)
            pe.wait_ge(self_in, 48)
            pe.wait_ge(xnT_ready, 2 * T)
            for m, w in enumerate((self_w[:, 0], self_w[:, 1])):
                for e in range(KIN):
                    for a in range(KIN):
                        ins = pe.matmul(BANK[4 + 2 * m + e], w[:, a, e * P:(e + 1) * P], xnT[:, a, :],
                                        start=(a == 0), stop=(a == KIN - 1))
                    ins.then_inc(qk2_ps, 1)
            pe.wait_ge(small_in, 64)
            for t in range(T):
                for a in range(KIN):
                    pe.matmul(BANK[t][:, 0:E], xnT[:, a, t * P:(t + 1) * P], self_w[:, 2, a, :], start=(a == 0), stop=False)
                pe.matmul(BANK[t][:, 0:E], ones_row[:], bias_v[:], start=False, stop=True).then_inc(v2_ps, 1)
            pe.wait_ge(qk2_ready, 2 * KIN)
            for t in range(T):
                for e in range(KIN):
                    ins = pe.matmul(BANK[4 + t][:, 0:P], q2T[:, e, t * P:(t + 1) * P], k2T[:, e, t * P:(t + 1) * P],
                                    start=(e == 0), stop=(e == KIN - 1))
                ins.then_inc(s2_ps, 1)
            for t in range(T):
                pe.wait_ge(p2_ready, t + 1)
                pe.wait_ge(v2_ready, t + 1)
                pe.transpose(BANK[t][:, 256:384], p2[:, t, :], ident[:]).then_inc(p2T_ps, 1)
            for t in range(T):
                pe.wait_ge(p2T_ready, t + 1)
                pe.matmul(BANK[4 + t][:, 256:512], p2T[:, t, :], v2[:, t, :], start=True, stop=True).then_inc(o2_ps, 1)
            transpose_xn(2, 0)
            pe.wait_ge(xnT_ready, 3 * T)
            for t in range(T):
                for a in range(KIN):
                    ins = pe.matmul(ps_m[:, t * NE:(t + 1) * NE], xnT[:, a, t * P:(t + 1) * P], w_g[:, a, :],
                                    start=(a == 0), stop=(a == KIN - 1))
            ins.then_inc(gate_ps, 1)

            def up(base, e):
                pe.wait_ge(up_split, base + (e + 1))
                for f in range(FT):
                    if e or f >= 2:
                        pe.wait_ge(hid_ready, base * FT + (FT * e + f - 1))
                    for m in range(2):
                        for a in range(KIN):
                            col = m * F + f * P
                            ins = product(BANK[2 * (f % 2) + m], up_high[:, e % 2, a, col:col + P],
                                          up_low[:, e % 2, a, col:col + P], xnT_high[:, a, :], xnT_low[:, a, :],
                                          a == 0, a == KIN - 1)
                    ins.then_inc(up_ps, 1)

            def down(base, e):
                pe.wait_ge(hid_split, base * FT + FT * (e + 1))
                pe.wait_ge(down_split, base + (e + 1))
                pe.wait_ge(summed, base * T + (T * e + 1))
                for t in range(T):
                    for f in range(FT):
                        cols = slice(t * P, (t + 1) * P)
                        ins = product(BANK[4 + t][:, 0:E], hid_high[:, e % 2, f, cols], hid_low[:, e % 2, f, cols],
                                      down_high[:, e % 2, f, :], down_low[:, e % 2, f, :], f == 0, f == FT - 1)
                    ins.then_inc(down_ps, 1)

            pe.wait_ge(xnT_split, 1)
            up(0, 0)
            pe.wait_ge(gate_sub, 1)
            with pe.Fori(0, NE // 2 - 1) as i:
                for j in range(2):
                    up(i * 2, j + 1)
                    down(i * 2, j)
            up(0, NE - 1)
            down(0, NE - 2)
            down(0, NE - 1)


def kernel(x, ctx_1024, mask_1x1xSxS2_bk0, L0_xattn_wq, L0_xattn_wk, L0_xattn_wv, L0_xattn_wo, L0_attn_Wq,
           L0_attn_bq, L0_attn_Wk, L0_attn_bk, L0_attn_Wv, L0_attn_bv, L0_ffn_gate_w, L0_ffn_gate_up_w,
           L0_ffn_down_w):
    import numpy as np
    import concourse.bacc as bacc
    from concourse.bass_utils import run_bass_kernel_spmd

    def turned(w):
        return np.asarray(w).T.reshape(KIN, P, E).transpose(1, 0, 2)

    mask = np.asarray(mask_1x1xSxS2_bk0).reshape(Q, S)
    units = mask.T.reshape(UNITS, UK, Q)
    turned_mask = np.concatenate([units[u] for u in PE_UNITS + INT_UNITS])
    chunks = np.asarray(ctx_1024).reshape(B * NC, CK, KIN, P).transpose(0, 3, 2, 1)
    ups = np.asarray(L0_ffn_gate_up_w).reshape(NE, KIN, P, 2 * F).transpose(0, 2, 1, 3)
    arrays = {
        "x": np.asarray(x).reshape(B * Q, E), "ctx_in": chunks, "mask_q": mask, "mask_k": turned_mask,
        "wq": turned(L0_xattn_wq), "wk": turned(L0_xattn_wk), "wv": turned(L0_xattn_wv), "wo": turned(L0_xattn_wo),
        "sq": turned(L0_attn_Wq), "bq": np.asarray(L0_attn_bq).reshape(KIN, P).T, "sk": turned(L0_attn_Wk), "bk": np.asarray(L0_attn_bk).reshape(KIN, P).T,
        "sv": turned(L0_attn_Wv), "bv": L0_attn_bv,
        "gate_w": L0_ffn_gate_w, "up_w": ups, "down_w": L0_ffn_down_w,
    }
    arrays = {name: np.ascontiguousarray(a) for name, a in arrays.items()}
    nc = bacc.Bacc("TRN2", target_bir_lowering=False, num_devices=1)
    args = {name: nc.dram_tensor(name, a.shape, mybir.dt.from_np(a.dtype), kind="ExternalInput").ap()
            for name, a in arrays.items()}
    out = nc.dram_tensor("out", (B * Q, E), F32, kind="ExternalOutput").ap()
    perceiver_block(nc, out=out, **args)
    got = run_bass_kernel_spmd(nc, [arrays], core_ids=[0])
    return got.results[0]["out"].reshape(B, Q, E)
```

```python
from contextlib import ExitStack

import concourse.bass as bass
from concourse import mybir

F32 = mybir.dt.float32
F32R = mybir.dt.float32r
BF16 = mybir.dt.bfloat16
I32 = mybir.dt.int32
U8 = mybir.dt.uint8
ALU = mybir.AluOpType
ACT = mybir.ActivationFunctionType
AX = mybir.AxisListType.X

P = 128
B, Q, E, S = 2, 256, 256, 4096
H, D = 16, 16
NH = B * H
T = B * Q // P
KIN = E // P
CK = 512
NC = S // CK
KT = S // P
UNITS = 8
UK = S // UNITS
UT = UK // P
STEPS = NH * UNITS
GROUP = 16
NE, F = 8, 512
FT = F // P
PARTS = 3
STACK = 6 * D
ROWS = STACK + PARTS
LEAD_A = 14
LEAD_B = 3
PE_UNITS = (5, 7)
DVE_UNITS = (2,)
POOL_UNITS = tuple(u for u in range(UNITS) if u not in PE_UNITS + DVE_UNITS)
PE_SLICE, DVE_SLICE, POOL_SLICE = (len(units) * UT * Q // NC for units in (PE_UNITS, DVE_UNITS, POOL_UNITS))
LATE, LATE_DVE_UNITS = STEPS - LEAD_A + 2, (1, 4, 6)
SLOTS = 4
LOADS = 6
BIG = 3.0e38
EPS = 1e-5


def masks(g):
    u = g % UNITS
    if u in PE_UNITS:
        return "pe"
    return "dve" if u in DVE_UNITS or (g >= LATE and u in LATE_DVE_UNITS) else "pool"


def masked(engine, g):
    return sum(masks(unit) == engine for unit in range(g + 1))


def perceiver_block(nc, x, ctx_in, mask_q, mask_k, wq, wk, wv, wo, sq, bq, sk, bk, sv, bv, gate_w, up_w, down_w, out):
    k_parts = nc.dram_tensor("k_parts", (PARTS, NH, D, S), BF16, kind="Internal").ap()
    q_parts = nc.dram_tensor("q_parts", (PARTS, NH, D, Q), BF16, kind="Internal").ap()

    with ExitStack() as ctx:
        def sb(name, shape, dt=F32):
            return ctx.enter_context(nc.sbuf_tensor(name, shape, dt))

        def sem(name):
            return ctx.enter_context(nc.semaphore(name))

        V = sb("V", [P, NH, KT, D])
        qst = sb("qst", [P, SLOTS, Q], BF16)
        xs = sb("xs", [P, T, E])
        xn = sb("xn", [P, T, E])
        xnT = sb("xnT", [P, KIN, B * Q])
        w_q = sb("w_q", [P, KIN, E])
        w_o = sb("w_o", [P, KIN, E])
        kp = sb("kp", [P, 2, 2, PARTS, CK], BF16)
        qp = sb("qp", [P, PARTS, KIN, B * Q], BF16)
        O = sb("O", [P, NH, Q // P, D + 1])
        norm = sb("norm", [P, NH, Q // P])
        any_kept = sb("any_kept", [P, NH, Q // P])
        ident = sb("ident", [P, P])
        ident_bf = sb("ident_bf", [P, P], BF16)
        fold = sb("fold", [P, 32])
        stats = sb("stats", [P, T, 6])
        mean_var = sb("mean_var", [P, T, 2])
        var_eps = sb("var_eps", [P, T])
        rstd = sb("rstd", [P, T])
        neg_half = sb("neg_half", [P, T])
        bias_qk = sb("bias_qk", [P, 2, KIN])
        bias_v = sb("bias_v", [1, E])
        ones_row = sb("ones_row", [1, P])
        group_bias = sb("group_bias", [P, P // GROUP, GROUP])
        w_g = sb("w_g", [P, KIN, NE])
        rank = sb("rank", [P, NE])
        lg = sb("lg", [P, 8, T, NE])
        tk = sb("tk", [P, 8, T])
        wgt = sb("wgt", [P, NE, T])

        with ExitStack() as phase:
            def of_phase(name, shape, dt=F32):
                return phase.enter_context(nc.sbuf_tensor(name, shape, dt))

            ctx_raw = of_phase("ctx_raw", [P, 2, KIN, CK])
            ctx_high = of_phase("ctx_high", [P, 2, KIN, CK], F32R)
            ctx_low = of_phase("ctx_low", [P, 2, KIN, CK], F32R)
            rest = of_phase("rest", [P, 2, CK])
            w_high = of_phase("w_high", [P, 2, KIN, E], F32R)
            w_low = of_phase("w_low", [P, 2, KIN, E], F32R)
        with ExitStack() as phase:
            def of_phase(name, shape, dt=F32):
                return phase.enter_context(nc.sbuf_tensor(name, shape, dt))

            kst_late = of_phase("kst_late", [P, 2, S], BF16)
            probs = of_phase("probs", [P, 4, UT * Q])
            Vh = of_phase("Vh", [P, 2, KT, 32])
            kst_early = of_phase("kst_early", [P, 2, S], BF16)
            mask_bias = of_phase("mask_bias", [P, Q // P, S], BF16)
            mask_turned = of_phase("mask_turned", [P, len(PE_UNITS), UT, Q], BF16)
            mask_keep = of_phase("mask_keep", [P, len(DVE_UNITS), UT, Q], BF16)
            mask_int = of_phase("mask_int", [P, len(POOL_UNITS), UT, Q], I32)
            unit_max = of_phase("unit_max", [P, 2, Q // P, UNITS])
            head_max = of_phase("head_max", [P, 2, Q // P])
            neg_parts = of_phase("neg_parts", [P, 2, Q // P, 4], BF16)
            neg_rest = of_phase("neg_rest", [P, 2, Q // P])
        kst = [kst_early[:, 0, :], kst_early[:, 1, :], kst_late[:, 0, :], kst_late[:, 1, :]]
        with ExitStack() as phase:
            def of_phase(name, shape, dt=F32):
                return phase.enter_context(nc.sbuf_tensor(name, shape, dt))

            xnT_high = of_phase("xnT_high", [P, KIN, B * Q], F32R)
            xnT_low = of_phase("xnT_low", [P, KIN, B * Q], F32R)
            up_high = of_phase("up_high", [P, 2, KIN, 2 * F], F32R)
            up_low = of_phase("up_low", [P, 2, KIN, 2 * F], F32R)
            down_high = of_phase("down_high", [P, 2, FT, E], F32R)
            down_low = of_phase("down_low", [P, 2, FT, E], F32R)
            hid_high = of_phase("hid_high", [P, 2, FT, B * Q], F32R)
            hid_low = of_phase("hid_low", [P, 2, FT, B * Q], F32R)

        V_flat = V[:].rearrange("p h k d -> p (h k d)")
        half = H * KT * D
        w_raw = V_flat[:, half:half + 2 * KIN * E].rearrange("p (w a n) -> p w a n", w=2, a=KIN)
        raw_q = V_flat[:, half + 2560:half + 4608].bitcast(U8).rearrange("p (t k) -> p t k", t=Q // P)
        raw_k = V_flat[:, half + 4608:half + 6656].bitcast(U8).rearrange("p (k q) -> p k q", k=KT)
        raw_k_flat = V_flat[:, half + 4608:half + 6656].bitcast(U8)
        mask_turned_flat, mask_keep_flat, mask_int_flat = (
            m[:].rearrange("p u k q -> p (u k q)") for m in (mask_turned, mask_keep, mask_int))
        oT = w_q
        unused = qp[:, 0]
        up_sb = V_flat[:, 0:2 * KIN * 2 * F].rearrange("p (s a n) -> p s a n", s=2, a=KIN)
        down_sb = V_flat[:, 4096:4096 + 2 * FT * E].rearrange("p (s a n) -> p s a n", s=2, a=FT)
        self_w = V_flat[:, 6144:6144 + 3 * KIN * E].rearrange("p (w a n) -> p w a n", w=3, a=KIN)
        at = half
        q2T = V_flat[:, at:at + 1024].rearrange("p (a t) -> p a t", a=KIN)
        k2T = V_flat[:, at + 1024:at + 2048].rearrange("p (a t) -> p a t", a=KIN)
        v2 = V_flat[:, at + 2048:at + 3072].rearrange("p (t e) -> p t e", t=T)
        attn = V_flat[:, at + 3072:at + 4096].rearrange("p (t e) -> p t e", t=T)
        aT = V_flat[:, at + 4096:at + 5120].rearrange("p (t e) -> p t e", t=T)
        s2 = V_flat[:, at + 5120:at + 5632].rearrange("p (t k) -> p t k", t=T)
        p2 = V_flat[:, at + 5632:at + 6144].rearrange("p (t k) -> p t k", t=T)
        p2T = V_flat[:, at + 6144:at + 6656].rearrange("p (t k) -> p t k", t=T)
        silu = V_flat[:, at + 6656:at + 7680].rearrange("p (s t) -> p s t", s=2)
        hid = V_flat[:, at:at + 1024].rearrange("p (s t) -> p s t", s=2)

        ps_a = ctx.enter_context(nc.psum_tensor("ps_a", [P, 2, 512], F32))
        ps_b = ctx.enter_context(nc.psum_tensor("ps_b", [P, 2, 1024], F32))
        ps_v = ctx.enter_context(nc.psum_tensor("ps_v", [P, 512], F32))
        ps_m = ctx.enter_context(nc.psum_tensor("ps_m", [P, 512], F32))
        BANK = [ps_a[:, 0, :], ps_a[:, 1, :], ps_b[:, 0, 0:512], ps_b[:, 0, 512:1024],
                ps_b[:, 1, 0:512], ps_b[:, 1, 512:1024], ps_v[:, :], ps_m[:, :]]
        max_rows = ps_m[STACK:STACK + PARTS, 0:Q]
        o_cols = ps_m[:, Q:Q + 64].rearrange("p (t d) -> p t d", t=2)

        x_in, wq_in, wk_in = (sem(n) for n in ("x_in", "wq_in", "wk_in"))
        wv_in, wo_in, small_in = (sem(n) for n in ("wv_in", "wo_in", "small_in"))
        mask_q_in, mask_k_in, self_in, out_done = (sem(n) for n in ("mask_q_in", "mask_k_in", "self_in", "out_done"))
        ctx_in_s = [sem(f"ctx_in{j}") for j in range(2)]
        k_out = [[sem(f"k_out{b}{j}") for j in range(2)] for b in range(B)]
        q_out = sem("q_out")
        stack_in = [sem(f"stack_in{j}") for j in range(SLOTS)]
        up_in = [sem(f"up_in{j}") for j in range(2)]
        down_in = [sem(f"down_in{j}") for j in range(2)]
        pool_consts, vh_set, consts = (sem(n) for n in ("pool_consts", "vh_set", "consts"))
        ones_set, dve_own = (sem(n) for n in ("ones_set", "dve_own"))
        var_ready, rstd_ready, xn_ready = (sem(n) for n in ("var_ready", "rstd_ready", "xn_ready"))
        xnT_ps, xnT_ready = (sem(n) for n in ("xnT_ps", "xnT_ready"))
        masks_ready = sem("masks_ready")
        k_ps, kh_ready, km_ready, v_ps = (sem(n) for n in ("k_ps", "kh_ready", "km_ready", "v_ps"))
        w_high_ready, w_split = (sem(n) for n in ("w_high_ready", "w_split"))
        ctx_high_ready, ctx_split = (sem(n) for n in ("ctx_high_ready", "ctx_split"))
        k_rest = sem("k_rest")
        kl_ready = [sem(f"kl_ready{e}") for e in range(2)]
        v_stored = [sem(f"v_stored{j}") for j in range(2)]
        q_ps, q_high, q_split = sem("q_ps"), sem("q_high"), sem("q_split")
        a_ps, tiles_seen, a_max, chain = (sem(n) for n in ("a_ps", "tiles_seen", "a_max", "chain"))
        neg_ready, rows_ps, rows_ready = (sem(n) for n in ("neg_ready", "rows_ps", "rows_ready"))
        b_ps, exp_done, pool_masked = (sem(n) for n in ("b_ps", "exp_done", "pool_masked"))
        dve_masked, pv_done, vh_ready = (sem(n) for n in ("dve_masked", "pv_done", "vh_ready"))
        oT_ready, o_ps, o_stored = sem("oT_ready"), sem("o_ps"), sem("o_stored")
        attn_ready, aT_ps, aT_ready, wo_ps = (sem(n) for n in ("attn_ready", "aT_ps", "aT_ready", "wo_ps"))
        qk2_ps, qk2_ready, v2_ps, v2_ready = (sem(n) for n in ("qk2_ps", "qk2_ready", "v2_ps", "v2_ready"))
        s2_ps, s2_ready, p2_ready = (sem(n) for n in ("s2_ps", "s2_ready", "p2_ready"))
        p2T_ps, p2T_ready, o2_ps = (sem(n) for n in ("p2T_ps", "p2T_ready", "o2_ps"))
        gate_ps, gate_sub, gate_exp = sem("gate_ps"), sem("gate_sub"), sem("gate_exp")
        xnT_high_ready, xnT_split = sem("xnT_high_ready"), sem("xnT_split")
        up_high_ready, up_split = (sem(n) for n in ("up_high_ready", "up_split"))
        down_high_ready, down_split = (sem(n) for n in ("down_high_ready", "down_split"))
        up_ps, silu_ready, hid_ready, hid_high_ready, hid_split, down_ps, summed = (sem(n) for n in (
            "up_ps", "silu_ready", "hid_ready", "hid_high_ready", "hid_split", "down_ps", "summed"))

        block = ctx.enter_context(nc.Block())

        def all_chunks(eng, chunk, after_first, after_q, before_last=lambda: None):
            with eng.Fori(0, NC // 2) as i:
                for c in range(2):
                    chunk(c, i)
            after_first()
            for c in range(NC, NC + 2):
                chunk(c, 0)
            after_q()
            with eng.Fori(0, NC // 2 - 2) as i:
                for c in range(NC + 2, NC + 4):
                    chunk(c, i)
            before_last()
            for c in range(2 * NC - 2, 2 * NC):
                chunk(c, 0)

        FIRST, LAST = UNITS, STEPS - 3 * UNITS
        EARLY = STEPS - 2

        def projected(t):
            return BANK[t][:, E:2 * E] if t < T // 2 else BANK[4 + t][:, 0:E]

        @block.sync
        def _(sp):
            for b in range(B):
                for j in range(2):
                    sp.sem_inc(k_out[b][j], 1)
            sp.dma_start(w_raw[:, 0], wk).then_inc(wk_in, 16)
            sp.dma_start(ctx_raw[:, 0], ctx_in[0]).then_inc(ctx_in_s[0], 16)
            sp.dma_start(w_raw[:, 1], wv).then_inc(wv_in, 16)
            sp.dma_start(ctx_raw[:, 1], ctx_in[1]).then_inc(ctx_in_s[1], 16)
            sp.dma_start(xs[:], x.rearrange("(t p) e -> p t e", p=P)).then_inc(x_in, 16)
            sp.dma_start(raw_k, mask_k).then_inc(mask_k_in, 16)
            sp.dma_start(raw_q, mask_q.rearrange("(t p) k -> p t k", p=P)).then_inc(mask_q_in, 16)
            sp.dma_start(w_q[:], wq).then_inc(wq_in, 16)
            sp.dma_start(w_o[:], wo).then_inc(wo_in, 16)
            sp.dma_start(bias_qk[:, 0, :], bq).then_inc(small_in, 16)
            sp.dma_start(bias_qk[:, 1, :], bk).then_inc(small_in, 16)
            sp.dma_start(bias_v[:], bv.rearrange("(o e) -> o e", o=1)).then_inc(small_in, 16)
            sp.dma_start(w_g[:], gate_w.rearrange("(a p) n -> p a n", p=P)).then_inc(small_in, 16)

            def serve_chunk(c, i):
                b, j = c // NC, c % 2
                if c < 2 * NC - 2:
                    sp.wait_ge(ctx_split, i * 2 + (c + 1))
                    sp.dma_start(ctx_raw[:, j], ctx_in[i * 2 + (c + 2)]).then_inc(ctx_in_s[j], 16)
                for e in range(2):
                    sp.wait_ge(kl_ready[e], i * 2 + (c + 2))
                    rows = k_parts[:, b * H + e * 8:b * H + e * 8 + 8].rearrange("a h d k -> (h d) a k")
                    keys = bass.ds(i * (2 * CK) + (c % NC) * CK, CK)
                    sp.dma_start(rows[:, :, keys], kp[:, j, e]).then_inc(k_out[b][j], 16)

            def load_stacks(n, slot):
                sp.dma_start(kst[slot][0:48, :], k_parts[0:3, n]).then_inc(stack_in[slot], 16)
                sp.dma_start(kst[slot][48:80, :], k_parts[0:2, n]).then_inc(stack_in[slot], 16)
                sp.dma_start(kst[slot][80:96, :], k_parts[0, n]).then_inc(stack_in[slot], 16)
                sp.dma_start(qst[0:48, slot, :], q_parts[0:1, n].broadcast_to([3, D, Q])).then_inc(stack_in[slot], 16)
                sp.dma_start(qst[48:80, slot, :], q_parts[1:2, n].broadcast_to([2, D, Q])).then_inc(stack_in[slot], 16)
                sp.dma_start(qst[80:96, slot, :], q_parts[2, n]).then_inc(stack_in[slot], 16)

            def serve_q():
                for e in range(KIN):
                    sp.wait_ge(q_split, e + 1)
                    for a in range(PARTS):
                        to = q_parts[a].rearrange("(b h) d q -> (h d) b q", b=B)[e * P:(e + 1) * P]
                        sp.dma_start(to, qp[:, a, e, :].rearrange("p (b q) -> p b q", b=B)).then_inc(q_out, 16)

            def load_first():
                sp.wait_ge(q_out, 16 * PARTS * KIN)
                for j in range(2):
                    sp.wait_ge(k_out[0][j], 16 * NC + 1)
                for n in range(2):
                    load_stacks(n, n)

            all_chunks(sp, serve_chunk, lambda: None, serve_q, load_first)
            sp.wait_ge(v_ps, 2 * B * NC)
            for j in range(2):
                sp.wait_ge(k_out[1][j], 16 * NC + 1)
            for n in range(2, SLOTS):
                load_stacks(n, n)
            with sp.Fori(0, NH // SLOTS - 1) as i:
                for slot in range(SLOTS):
                    n = sp.snap(i * SLOTS + (SLOTS + slot))
                    sp.wait_ge(b_ps, i * (SLOTS * UNITS) + (slot + 1) * UNITS)
                    load_stacks(n, slot)

            def load_up(e, s):
                sp.dma_start(up_sb[:, s], up_w[e]).then_inc(up_in[s], 16)

            def load_down(e, s):
                sp.dma_start(down_sb[:, s], down_w[e].rearrange("(a p) n -> p a n", p=P)).then_inc(down_in[s], 16)

            sp.wait_ge(vh_ready, H)
            for e in range(2):
                load_up(e, e)
                load_down(e, e)
            for m, w in enumerate((sq, sk, sv)):
                sp.dma_start(self_w[:, m], w).then_inc(self_in, 16)
            with sp.Fori(0, NE // 2 - 1) as i:
                for s in range(2):
                    e = sp.snap(i * 2 + (s + 2))
                    sp.wait_ge(up_split, i * 2 + (s + 1))
                    load_up(e, s)
                    sp.wait_ge(down_split, i * 2 + (s + 1))
                    load_down(e, s)
            sp.wait_ge(summed, NE * T + 1)
            sp.dma_start(out.rearrange("(t p) e -> p t e", p=P), xs[:]).then_inc(out_done, 16)
            sp.wait_ge(out_done, 16)

        @block.gpsimd
        def _(pool):
            for e in range(2):
                pool.sem_inc(kl_ready[e], 1)
            pool.memset(neg_half[:], -0.5).then_inc(pool_consts, 1)
            pool.memset(ident[:], 0.0).then_inc(pool_consts, 1)
            pool.memset(fold[:], 0.0).then_inc(pool_consts, 1)
            pool.memset(group_bias[:], 0.0).then_inc(pool_consts, 1)
            pool.wait_ge(pool_consts, 4)
            pool.affine_select(out=ident[:], in_=ident[:], compare_op=ALU.not_equal, fill=1.0, base=0,
                               pattern=[[-1, P]], channel_multiplier=1).then_inc(consts, 1)

            def rstds(n):
                pool.wait_ge(var_ready, n + 1)
                pool.tensor_tensor(rstd[:], var_eps[:], neg_half[:], ALU.pow).then_inc(rstd_ready, 1)

            pool.wait_ge(consts, 1)
            pool.memset(kst_early[STACK:ROWS, :, :], 1.0).then_inc(ones_set, 1)
            pool.wait_ge(ones_set, 1)
            rstds(0)
            for g in range(4):
                pool.affine_select(out=fold[:], in_=fold[:], compare_op=ALU.not_equal, fill=1.0, base=-32 * g,
                                   pattern=[[-1, 32]], channel_multiplier=1).then_inc(pool_consts, 1)
                pool.wait_ge(pool_consts, 5 + g)
            pool.affine_select(out=group_bias[:], in_=group_bias[:], compare_op=ALU.is_ge, fill=-BIG, base=0,
                               pattern=[[-GROUP, P // GROUP], [0, GROUP]], channel_multiplier=1).then_inc(pool_consts, 1)
            pool.wait_ge(pool_consts, 9)
            pool.affine_select(out=group_bias[:], in_=group_bias[:], compare_op=ALU.is_ge, fill=-BIG, base=GROUP - 1,
                               pattern=[[GROUP, P // GROUP], [0, GROUP]], channel_multiplier=-1).then_inc(consts, 1)
            pool.wait_ge(consts, 3)

            with pool.Fori(0, B * NC // 2) as i:
                for j in range(2):
                    for e in range(2):
                        pool.wait_ge(km_ready, i * 4 + (2 * j + e + 1))
                        pool.tensor_tensor(kp[:, j, e, 2, :], rest[:, e, :], kp[:, j, e, 1, :],
                                           ALU.subtract).then_inc(kl_ready[e], 1)
            pool.wait_ge(v_ps, 2 * B * NC)
            for e in range(2):
                pool.wait_ge(kl_ready[e], B * NC + 1)
            pool.memset(Vh[:], 0.0).then_inc(vh_set, 1)
            pool.wait_ge(vh_set, 1)
            pool.memset(Vh[:, :, :, D:D + 1], 1.0).then_inc(vh_set, 1)
            pool.wait_ge(vh_set, 2)
            pool.memset(kst_late[STACK:ROWS, :, :], 1.0).then_inc(ones_set, 1)
            pool.wait_ge(ones_set, 2)

            pool.wait_ge(masks_ready, 4 * NC)

            def mask_unit(heads, g):
                pool.wait_ge(exp_done, heads * UNITS + (g + 1))
                tile = probs[:, g % 4, :]
                keep = mask_int[:, POOL_UNITS.index(g % UNITS)].rearrange("p k q -> p (k q)")
                pool.tensor_tensor(tile.bitcast(I32), tile.bitcast(I32), keep, ALU.mult).then_inc(pool_masked, 1)

            with pool.Fori(0, LATE // UNITS) as n:
                for u in POOL_UNITS:
                    mask_unit(n, u)
            for g in range(LATE // UNITS * UNITS, STEPS):
                if masks(g) == "pool":
                    mask_unit(0, g)
            rstds(1)

            def low_weights(base, e):
                s = e % 2
                pool.wait_ge(up_high_ready, base + (e + 1))
                pool.tensor_tensor(up_low[:, s], up_sb[:, s], up_high[:, s].bitcast(F32),
                                   ALU.subtract).then_inc(up_split, 1)
                pool.wait_ge(down_high_ready, base + (e + 1))
                pool.tensor_tensor(down_low[:, s], down_sb[:, s], down_high[:, s].bitcast(F32),
                                   ALU.subtract).then_inc(down_split, 1)

            low_weights(0, 0)
            rstds(2)
            low_weights(0, 1)
            with pool.Fori(0, NE // 2 - 1) as i:
                for j in range(2):
                    low_weights(i * 2, j + 2)

        @block.scalar
        def _(act):
            act.wait_ge(consts, 1)
            act.activation(ident_bf[:], ident[:], ACT.Copy).then_inc(consts, 1)

            def high_chunk(c, i):
                j = c % 2
                act.wait_ge(ctx_in_s[j], i * 16 + 16 * (c // 2 + 1))
                act.activation(ctx_high[:, j], ctx_raw[:, j], ACT.Copy).then_inc(ctx_high_ready, 1)

            def split_k(c, i):
                b, j = c // NC, c % 2
                if c in (NC, NC + 1):
                    act.wait_ge(k_out[0][j], 16 * NC + 1)
                else:
                    act.wait_ge(k_out[b][j], i * 32 + (32 * (c % NC // 2) + 1))
                for e in range(2):
                    act.wait_ge(k_ps, i * 4 + (2 * c + e + 1))
                    act.activation(kp[:, j, e, 0, :], BANK[e], ACT.Copy).then_inc(kh_ready, 1)
                for e in range(2):
                    act.wait_ge(k_rest, i * 4 + (2 * c + e + 2))
                    act.activation(kp[:, j, e, 1, :], rest[:, e, :], ACT.Copy).then_inc(km_ready, 1)
                if b == 0:
                    act.wait_ge(mask_k_in, 16)
                    at = i * (2 * POOL_SLICE) + c * POOL_SLICE
                    part = bass.ds(at, POOL_SLICE)
                    raw = bass.ds(at + len(PE_UNITS + DVE_UNITS) * UT * Q, POOL_SLICE)
                    act.activation(mask_int_flat[:, part], raw_k_flat[:, raw], ACT.Copy).then_inc(masks_ready, 1)
                if c < 2 * NC - 2:
                    act.wait_ge(v_ps, i * 4 + 2 * (c + 1))
                    high_chunk(c + 2, i)

            for w, arrived in enumerate((wk_in, wv_in)):
                act.wait_ge(arrived, 16)
                act.activation(w_high[:, w], w_raw[:, w], ACT.Copy).then_inc(w_high_ready, 1)
                high_chunk(w, 0)

            def turn_x():
                for k in range(T // 2):
                    act.wait_ge(xnT_ps, 2 * (k + 1))
                    act.activation(xnT[:, :, k * 2 * P:(k + 1) * 2 * P].rearrange("p a (t q) -> p t a q", t=2),
                                   BANK[6 + k].rearrange("p (t a q) -> p t a q", t=2, a=KIN), ACT.Copy).then_inc(xnT_ready, 2)

            def high_q():
                for e in range(KIN):
                    act.wait_ge(q_ps, e + 1)
                    act.activation(qp[:, 0, e, :], BANK[6 + e], ACT.Copy, scale=float(D) ** -0.5).then_inc(q_high, 1)

            all_chunks(act, split_k, turn_x, high_q)

            def copy_xnT(n):
                for t in range(T):
                    act.wait_ge(xnT_ps, T * n + t + 1)
                    act.activation(xnT[:, :, t * P:(t + 1) * P],
                                   BANK[t][:, 0:E].rearrange("p (a q) -> p a q", a=KIN), ACT.Copy).then_inc(xnT_ready, 1)

            def copy_aT(first, last):
                for t in range(first, last):
                    act.wait_ge(aT_ps, t + 1)
                    act.activation(aT[:, t, :], BANK[t][:, 0:E], ACT.Copy).then_inc(aT_ready, 1)

            def copy_vh(n, p):
                act.activation(Vh[:, p, :, 0:D], V[:, n], ACT.Copy).then_inc(vh_ready, 1)

            def exp_unit(base, g):
                act.wait_ge(b_ps, base + g + 1)
                if g >= 4:
                    act.wait_ge(pv_done, base + (g - 3))
                act.activation(probs[:, g % 4, :], ps_b[:, g % 2, :], ACT.Exp).then_inc(exp_done, 1)

            def copy_rows(base, n):
                act.wait_ge(rows_ps, base + n + 1)
                act.activation(qst[STACK:ROWS, n % SLOTS, :], max_rows, ACT.Copy).then_inc(rows_ready, 1)

            def copy_oT(base, n):
                act.wait_ge(pv_done, base * UNITS + UNITS * (n + 1))
                if n >= 2:
                    act.wait_ge(o_ps, base + (n - 1))
                act.activation(oT[:, n % 2, :], ps_v[:, 0:Q], ACT.Copy).then_inc(oT_ready, 1)

            for b in range(2):
                act.wait_ge(v_stored[b], 2 * NC + 1)
            for e in range(2):
                act.wait_ge(kl_ready[e], B * NC + 1)
            copy_rows(0, 0)
            for g in range(LEAD_B):
                exp_unit(0, g)
            act.wait_ge(vh_set, 2)
            copy_vh(0, 0)

            def step(base, heads, s):
                if s % UNITS == 0 and s > 0:
                    copy_oT(heads, s // UNITS - 1)
                if s % UNITS == 4 and s // UNITS + 1 < NH:
                    copy_rows(heads, s // UNITS + 1)
                if s + LEAD_B < STEPS:
                    exp_unit(base, s + LEAD_B)
                if s % UNITS == 6 and s // UNITS + 1 < NH:
                    n = s // UNITS + 1
                    if n >= 2:
                        act.wait_ge(pv_done, base + UNITS * (n - 1))
                    copy_vh(heads + n, n % 2)


            for s in range(FIRST):
                step(0, 0, s)
            body = SLOTS * UNITS
            with act.Fori(0, (LAST - FIRST) // body) as i:
                for s in range(FIRST, FIRST + body):
                    step(i * body, i * SLOTS, s)
            for s in range(LAST, STEPS):
                step(0, 0, s)
            copy_oT(0, NH - 1)

            def high_up(base, e):
                s = e % 2
                act.wait_ge(up_in[s], base * 8 + 16 * (e // 2 + 1))
                if e >= 2:
                    act.wait_ge(up_ps, base * FT + FT * (e - 1))
                act.activation(up_high[:, s], up_sb[:, s], ACT.Copy).then_inc(up_high_ready, 1)

            def high_down(base, e):
                s = e % 2
                act.wait_ge(down_in[s], base * 8 + 16 * (e // 2 + 1))
                if e >= 2:
                    act.wait_ge(down_ps, base * T + T * (e - 1))
                act.activation(down_high[:, s], down_sb[:, s], ACT.Copy).then_inc(down_high_ready, 1)

            copy_aT(0, T // 2)
            copy_aT(T // 2, T)
            high_up(0, 0)
            high_down(0, 0)
            copy_xnT(1)
            act.wait_ge(small_in, 64)
            for m, to in enumerate((q2T, k2T)):
                for e in range(KIN):
                    act.wait_ge(qk2_ps, 2 * m + e + 1)
                    act.activation(to[:, e, :], BANK[4 + 2 * m + e], ACT.Identity,
                                   bias=bias_qk[:, m, e:e + 1]).then_inc(qk2_ready, 1)
            for t in range(T):
                act.wait_ge(s2_ready, t + 1)
                act.activation(p2[:, t, :], s2[:, t, :], ACT.Exp, bias=tk[:, 1, t:t + 1],
                               accum_out=tk[:, 2, t:t + 1]).then_inc(p2_ready, 1)
            for t in range(T):
                act.wait_ge(p2T_ps, t + 1)
                act.activation(p2T[:, t, :], BANK[t][:, 256:384], ACT.Copy).then_inc(p2T_ready, 1)
            high_up(0, 1)
            high_down(0, 1)
            for t in range(T):
                act.wait_ge(xnT_ps, 2 * T + t + 1)
                at = slice(t * P, (t + 1) * P)
                act.activation(xnT[:, :, at], BANK[4 + t][:, 0:E].rearrange("p (a q) -> p a q", a=KIN),
                               ACT.Copy).then_inc(xnT_ready, 1)
                act.wait_ge(xnT_ready, 2 * T + t + 1)
                act.activation(xnT_high[:, :, at], xnT[:, :, at], ACT.Copy).then_inc(xnT_high_ready, 1)
            act.wait_ge(gate_sub, 1)
            act.activation(lg[:, 1], lg[:, 0], ACT.Exp).then_inc(gate_exp, 1)

            def gates(base, e):
                for f in range(FT):
                    act.wait_ge(up_ps, base * FT + (FT * e + f + 1))
                    act.activation(silu[:, f % 2, :], BANK[2 * (f % 2)], ACT.Silu).then_inc(silu_ready, 1)
                    act.wait_ge(hid_ready, base * FT + (FT * e + f + 1))
                    act.activation(hid_high[:, e % 2, f, :], hid[:, f % 2, :], ACT.Copy).then_inc(hid_high_ready, 1)

            gates(0, 0)
            with act.Fori(0, NE // 2 - 1) as i:
                for j in range(2):
                    high_up(i * 2, j + 2)
                    gates(i * 2, j + 1)
                    high_down(i * 2, j + 2)
            gates(0, NE - 1)

        @block.vector
        def _(dve):
            count = [0]

            def link(ins):
                count[0] += 1
                ins.then_inc(dve_own, 1)
                dve.wait_ge(dve_own, count[0])

            def mark(ins):
                count[0] += 1
                ins.then_inc(dve_own, 1)

            def tile_stats(first, last, update=None):
                done = {}
                for t in range(first, last + 2):
                    if t < last and update:
                        mark(update(t))
                        done["xs", t] = count[0]
                    if first < t <= last:
                        if update:
                            dve.wait_ge(dve_own, done["xs", t - 1])
                        mark(dve.bn_stats(stats[:, t - 1, :], xs[:, t - 1, :]))
                        done["stats", t - 1] = count[0]
                    if t >= first + 2:
                        dve.wait_ge(dve_own, done["stats", t - 2])
                        mark(dve.bn_aggr(mean_var[:, t - 2, :], stats[:, t - 2, :]))

            def layer_norm(n):
                dve.wait_ge(dve_own, count[0])
                dve.tensor_scalar(var_eps[:], mean_var[:, :, 1], EPS, None, ALU.add).then_inc(var_ready, 1)
                dve.wait_ge(rstd_ready, n + 1)
                for t in range(T):
                    dve.tensor_scalar(xn[:, t, :], xs[:, t, :], mean_var[:, t, 0:1], rstd[:, t:t + 1],
                                      ALU.subtract, ALU.mult).then_inc(xn_ready, 1)

            for j in range(2):
                dve.sem_inc(v_stored[j], 1)
            dve.sem_inc(k_rest, 1)
            dve.sem_inc(summed, 1)
            def low_chunk(c, i):
                dve.wait_ge(ctx_high_ready, i * 2 + (c + 1))
                dve.tensor_tensor(ctx_low[:, c % 2], ctx_raw[:, c % 2], ctx_high[:, c % 2].bitcast(F32),
                                  ALU.subtract).then_inc(ctx_split, 1)

            def store_kv(c, i):
                b, j = c // NC, c % 2
                for e in range(2):
                    dve.wait_ge(kh_ready, i * 4 + (2 * c + e + 1))
                    dve.wait_ge(kl_ready[e], i * 2 + (c + 1))
                    dve.tensor_tensor(rest[:, e, :], BANK[e], kp[:, j, e, 0, :],
                                      ALU.subtract).then_inc(k_rest, 1)
                for v in range(2):
                    dve.wait_ge(v_ps, i * 4 + (2 * c + v + 1))
                    to = V[:, b * H:(b + 1) * H, bass.ds(i * 8 + (4 * (c % NC) + 2 * v), 2), :]
                    dve.tensor_copy(to, BANK[2 + 2 * j + v].rearrange("p (k h d) -> p h k d", k=2, h=H)
                                    ).then_inc(v_stored[j], 1)
                if c < 2 * NC - 2:
                    low_chunk(c + 2, i)
                if b == 0:
                    dve.wait_ge(mask_k_in, 16)
                    part = bass.ds(i * (2 * PE_SLICE) + c * PE_SLICE, PE_SLICE)
                    dve.tensor_scalar(mask_turned_flat[:, part], raw_k_flat[:, part], BIG, -BIG, ALU.mult,
                                      ALU.add).then_inc(masks_ready, 1)
                    at = i * (2 * DVE_SLICE) + c * DVE_SLICE
                    part = bass.ds(at, DVE_SLICE)
                    raw = bass.ds(at + len(PE_UNITS) * UT * Q, DVE_SLICE)
                    dve.tensor_copy(mask_keep_flat[:, part], raw_k_flat[:, raw]).then_inc(masks_ready, 1)
                    dve.wait_ge(mask_q_in, 16)
                    keys = bass.ds(i * (2 * CK) + c * CK, CK)
                    dve.tensor_scalar(mask_bias[:, :, keys], raw_q[:, :, keys], BIG, -BIG, ALU.mult,
                                      ALU.add).then_inc(masks_ready, 1)

            for w in range(2):
                dve.wait_ge(w_high_ready, w + 1)
                dve.tensor_tensor(w_low[:, w], w_raw[:, w], w_high[:, w].bitcast(F32),
                                  ALU.subtract).then_inc(w_split, 1)
                low_chunk(w, 0)
            dve.wait_ge(x_in, 16)
            tile_stats(0, T)
            layer_norm(0)

            def split_q():
                for e in range(KIN):
                    dve.wait_ge(q_high, e + 1)
                    rest_q = xn[:, 2 * e:2 * e + 2, :].rearrange("p t e -> p (t e)")
                    link(dve.scalar_tensor_tensor(rest_q, BANK[6 + e], float(D) ** -0.5, qp[:, 0, e, :],
                                                  ALU.mult, ALU.subtract))
                    link(dve.tensor_copy(qp[:, 1, e, :], rest_q))
                    dve.tensor_tensor(qp[:, 2, e, :], rest_q, qp[:, 1, e, :], ALU.subtract).then_inc(q_split, 1)

            all_chunks(dve, store_kv, lambda: dve.wait_ge(masks_ready, 4 * NC), split_q)
            for n in range(NE):
                ins = dve.memset(rank[:, n:n + 1], float(NE - n))
            mark(ins)
            mark(dve.memset(ones_row[:], 1.0))
            def maxima(base, a, t):
                u, n = a % UNITS, a // UNITS
                dve.wait_ge(a_ps, base * 2 + (2 * a + t + 1))
                dve.sem_inc(tiles_seen, 1)
                dve.tensor_tensor_reduce(unused[:, t, :], ps_a[:, t, :], mask_bias[:, t, u * UK:(u + 1) * UK],
                                         1.0, -BIG, ALU.add, ALU.max,
                                         unit_max[:, n % 2, t, u:u + 1]).then_inc(a_max, 1)

            def negate_max(heads, n, part):
                p = n % 2
                if part == 0:
                    dve.wait_ge(a_max, heads * 16 + 16 * (n + 1))
                    dve.tensor_reduce(head_max[:, p, :], unit_max[:, p], AX, ALU.max).then_inc(chain, 1)
                    return
                dve.wait_ge(chain, heads * 4 + (4 * n + part))
                if part == 1:
                    dve.tensor_scalar(any_kept[:, heads + n, :], head_max[:, p, :], -1e38, None, ALU.is_gt)
                    dve.tensor_scalar(neg_parts[:, p, :, 0], head_max[:, p, :], -1.0, None, ALU.mult).then_inc(chain, 1)
                elif part == 2:
                    dve.scalar_tensor_tensor(neg_rest[:, p, :], head_max[:, p, :], -1.0, neg_parts[:, p, :, 0],
                                             ALU.mult, ALU.subtract).then_inc(chain, 1)
                elif part == 3:
                    dve.tensor_copy(neg_parts[:, p, :, 1], neg_rest[:, p, :]).then_inc(chain, 1)
                else:
                    dve.tensor_tensor(neg_parts[:, p, :, 2], neg_rest[:, p, :], neg_parts[:, p, :, 1],
                                      ALU.subtract).then_inc(neg_ready, 1)

            def mask_unit(base, g, part):
                u = g % UNITS
                keep = mask_keep[:, DVE_UNITS.index(u)] if u in DVE_UNITS else mask_int[:, POOL_UNITS.index(u)]
                cols = slice(part * UT * Q // 2, (part + 1) * UT * Q // 2)
                if part == 0:
                    dve.wait_ge(exp_done, base + g + 1)
                dve.scalar_tensor_tensor(probs[:, g % 4, cols], probs[:, g % 4, cols], BIG,
                                         keep.rearrange("p k q -> p (k q)")[:, cols], ALU.min,
                                         ALU.mult).then_inc(dve_masked, 1)

            def store_o(heads, n):
                dve.wait_ge(o_ps, heads + n + 1)
                dve.tensor_copy(O[:, heads + n, :, :], o_cols[:, :, 0:D + 1]).then_inc(o_stored, 1)

            def normalise(b):
                heads = slice(b * H, (b + 1) * H)
                kept = any_kept[:, heads, :]
                dve.wait_ge(o_stored, (b + 1) * H)
                link(dve.tensor_tensor(norm[:, heads, :], O[:, heads, :, D], kept, ALU.mult))
                link(dve.reciprocal(norm[:, heads, :], norm[:, heads, :]))
                link(dve.tensor_tensor(norm[:, heads, :], norm[:, heads, :], kept, ALU.mult))
                for t in range(2):
                    dve.tensor_tensor(attn[:, 2 * b + t, :].rearrange("p (h d) -> p h d", h=H),
                                      O[:, heads, t, 0:D], norm[:, heads, t:t + 1].broadcast_to([P, H, D]),
                                      ALU.mult).then_inc(attn_ready, 1)

            def add_attention(t):
                dve.wait_ge(wo_ps, t + 1)
                return dve.tensor_tensor(xs[:, t, :], xs[:, t, :], projected(t), ALU.add)

            for a in range(LEAD_A):
                for t in range(2):
                    maxima(0, a, t)
                    part = 2 * a + t - (2 * UNITS - 1)
                    if 0 <= part < 5:
                        negate_max(0, 0, part)

            def step(base, heads, s):
                for t in range(2):
                    if s + LEAD_A < STEPS:
                        maxima(base, s + LEAD_A, t)
                    part = 2 * (s % UNITS) + t - 3
                    if 0 <= part < 5 and s // UNITS + 1 < NH:
                        negate_max(heads, s // UNITS + 1, part)
                    g = s + 1 + t
                    if g < STEPS and masks(g) == "dve":
                        mask_unit(base, g, 1 - t)
                if s % UNITS == 2 and s >= UNITS:
                    store_o(heads, s // UNITS - 1)
                if s == EARLY:
                    dve.wait_ge(vh_ready, NH)
                    normalise(0)

            for s in range(FIRST):
                step(0, 0, s)
            with dve.Fori(0, (LAST - FIRST) // (2 * UNITS)) as i:
                for s in range(FIRST, FIRST + 2 * UNITS):
                    step(i * (2 * UNITS), i * 2, s)
            for s in range(LAST, STEPS):
                step(0, 0, s)
            store_o(0, NH - 1)
            normalise(1)
            tile_stats(0, T, add_attention)
            layer_norm(1)
            def copy_values(tiles):
                for t in tiles:
                    dve.wait_ge(v2_ps, t + 1)
                    dve.tensor_copy(v2[:, t, :], BANK[t][:, 0:E]).then_inc(v2_ready, 1)

            copy_values(range(T // 2))
            group_b = group_bias[:].rearrange("p a b -> p (a b)")
            dve.wait_ge(consts, 3)
            for t in range(T):
                dve.wait_ge(s2_ps, t + 1)
                link(dve.tensor_tensor_reduce(s2[:, t, :], BANK[4 + t][:, 0:P], group_b, 1.0, -BIG,
                                              ALU.add, ALU.max, tk[:, 0, t:t + 1]))
                dve.tensor_scalar(tk[:, 1, t:t + 1], tk[:, 0, t:t + 1], -1.0, None, ALU.mult).then_inc(s2_ready, 1)
            copy_values(range(T // 2, T))
            dve.wait_ge(p2_ready, T)
            link(dve.reciprocal(tk[:, 3, :], tk[:, 2, :]))

            def add_self_attention(t):
                dve.wait_ge(o2_ps, t + 1)
                return dve.scalar_tensor_tensor(xs[:, t, :], BANK[4 + t][:, 256:512], tk[:, 3, t:t + 1], xs[:, t, :],
                                                ALU.mult, ALU.add)

            tile_stats(0, T, add_self_attention)
            layer_norm(2)

            for t in range(T):
                dve.wait_ge(xnT_high_ready, t + 1)
                at = slice(t * P, (t + 1) * P)
                dve.tensor_tensor(xnT_low[:, :, at], xnT[:, :, at], xnT_high[:, :, at].bitcast(F32),
                                  ALU.subtract).then_inc(xnT_split, 1)

            def wide(col):
                return col.rearrange("p (t o) -> p t o", o=1).broadcast_to([P, T, NE])

            ranks = rank[:].rearrange("p (o n) -> p o n", o=1).broadcast_to([P, T, NE])
            logits = ps_m[:, 0:T * NE].rearrange("p (t n) -> p t n", t=T)
            dve.wait_ge(gate_ps, 1)
            link(dve.tensor_reduce(tk[:, 4, :], logits, AX, ALU.max))
            dve.tensor_tensor(lg[:, 0], logits, wide(tk[:, 4, :]), ALU.subtract).then_inc(gate_sub, 1)

            def softmax():
                dve.wait_ge(gate_exp, 1)
                link(dve.tensor_reduce(tk[:, 5, :], lg[:, 1], AX, ALU.add))
                link(dve.reciprocal(tk[:, 5, :], tk[:, 5, :]))
                link(dve.tensor_tensor(lg[:, 2], lg[:, 1], wide(tk[:, 5, :]), ALU.mult))

            def pick(values, best, chosen):
                link(dve.tensor_reduce(tk[:, best, :], values, AX, ALU.max))
                link(dve.tensor_tensor(lg[:, 3], values, wide(tk[:, best, :]), ALU.is_equal))
                link(dve.tensor_tensor(lg[:, 3], lg[:, 3], ranks, ALU.mult))
                link(dve.tensor_reduce(tk[:, 4, :], lg[:, 3], AX, ALU.max))
                link(dve.tensor_tensor(chosen, lg[:, 3], wide(tk[:, 4, :]), ALU.is_equal))

            def pick_first():
                pick(lg[:, 2], 6, lg[:, 4])
                link(dve.scalar_tensor_tensor(lg[:, 5], lg[:, 4], -2.0, lg[:, 2], ALU.mult, ALU.add))

            def expert_weights():
                link(dve.tensor_tensor(tk[:, 5, :], tk[:, 6, :], tk[:, 7, :], ALU.add))
                link(dve.reciprocal(tk[:, 5, :], tk[:, 5, :]))
                link(dve.tensor_tensor(lg[:, 4], lg[:, 4], lg[:, 6], ALU.add))
                link(dve.tensor_tensor(lg[:, 4], lg[:, 4], lg[:, 2], ALU.mult))
                link(dve.tensor_tensor(wgt[:].rearrange("p n t -> p t n"), lg[:, 4], wide(tk[:, 5, :]), ALU.mult))

            def hidden(base, e, beside=()):
                for f in range(FT):
                    dve.wait_ge(silu_ready, base * FT + (FT * e + f + 1))
                    dve.tensor_tensor(hid[:, f % 2, :], silu[:, f % 2, :], BANK[2 * (f % 2) + 1],
                                      ALU.mult).then_inc(hid_ready, 1)
                    dve.wait_ge(hid_high_ready, base * FT + (FT * e + f + 1))
                    dve.tensor_tensor(hid_low[:, e % 2, f, :], hid[:, f % 2, :], hid_high[:, e % 2, f, :].bitcast(F32),
                                      ALU.subtract).then_inc(hid_split, 1)
                    if beside:
                        beside[f]()

            def add_expert(base, e):
                for t in range(T):
                    dve.wait_ge(down_ps, base * T + (T * e + t + 1))
                    dve.scalar_tensor_tensor(xs[:, t, :], BANK[4 + t][:, 0:E], wgt[:, base + e, t:t + 1],
                                             xs[:, t, :], ALU.mult, ALU.add).then_inc(summed, 1)

            hidden(0, 0, (softmax, pick_first, lambda: pick(lg[:, 5], 7, lg[:, 6]), expert_weights))
            with dve.Fori(0, NE // 2 - 1) as i:
                for j in range(2):
                    hidden(i * 2, j + 1)
                    add_expert(i * 2, j)
            hidden(0, NE - 1)
            add_expert(0, NE - 2)
            add_expert(0, NE - 1)

        @block.tensor
        def _(pe):
            def transpose_xn(n, first_bank):
                for t in range(T):
                    pe.wait_ge(xn_ready, T * n + t + 1)
                    for a in range(KIN):
                        ins = pe.transpose(BANK[first_bank + t][:, a * P:(a + 1) * P], xn[:, t, a * P:(a + 1) * P],
                                           ident[:])
                    ins.then_inc(xnT_ps, 1)

            def product(out, high, low, to_high, to_low, start, stop):
                pe.matmul(out, high, to_high, start=start, stop=False)
                pe.matmul(out, high, to_low, start=False, stop=False)
                return pe.matmul(out, low, to_high, start=False, stop=stop)

            def project_kv(c, i):
                j = c % 2
                pe.wait_ge(ctx_split, i * 2 + (c + 1))
                pe.wait_ge(k_rest, i * 4 + (2 * c + 1))
                for e in range(2):
                    for a in range(KIN):
                        cols = slice(e * P, (e + 1) * P)
                        ins = product(BANK[e], w_high[:, 0, a, cols], w_low[:, 0, a, cols],
                                      ctx_high[:, j, a, :], ctx_low[:, j, a, :], a == 0, a == KIN - 1)
                    ins.then_inc(k_ps, 1)
                pe.wait_ge(w_split, 2)
                pe.wait_ge(v_stored[j], i * 2 + (2 * (c // 2) + 1))
                for v in range(2):
                    for k in range(2):
                        for a in range(KIN):
                            keys = slice((2 * v + k) * P, (2 * v + k + 1) * P)
                            ins = product(BANK[2 + 2 * j + v][:, k * E:(k + 1) * E],
                                          ctx_high[:, j, a, keys], ctx_low[:, j, a, keys],
                                          w_high[:, 1, a, :], w_low[:, 1, a, :], a == 0, a == KIN - 1)
                    ins.then_inc(v_ps, 1)

            def turn_x():
                for t in range(T):
                    pe.wait_ge(xn_ready, t + 1)
                    for a in range(KIN):
                        at = ((t % 2) * KIN + a) * P
                        ins = pe.transpose(BANK[6 + t // 2][:, at:at + P], xn[:, t, a * P:(a + 1) * P], ident[:])
                    ins.then_inc(xnT_ps, 1)

            def project_q():
                pe.wait_ge(wq_in, 16)
                pe.wait_ge(xnT_ready, T)
                for e in range(KIN):
                    for a in range(KIN):
                        ins = pe.matmul(BANK[6 + e], w_q[:, a, e * P:(e + 1) * P], xnT[:, a, :],
                                        start=(a == 0), stop=(a == KIN - 1))
                    ins.then_inc(q_ps, 1)

            pe.wait_ge(w_split, 1)
            pe.wait_ge(consts, 1)
            all_chunks(pe, project_kv, turn_x, project_q)

            def scores_for_max(base, a, t):
                n, u = a // UNITS, a % UNITS
                slot = n % SLOTS
                if u == 0 and t == 0:
                    pe.wait_ge(stack_in[slot], base * (16 * LOADS // (SLOTS * UNITS)) + 16 * LOADS * (n // SLOTS + 1))
                if a >= 1:
                    pe.wait_ge(a_max, base * 2 + (2 * a + t - 1))
                pe.matmul(ps_a[:, t, :], qst[0:STACK, slot, t * P:(t + 1) * P],
                          kst[slot][0:STACK, u * UK:(u + 1) * UK], start=True, stop=True).then_inc(a_ps, 1)

            def turn_max(heads, n):
                pe.wait_ge(neg_ready, heads + n + 1)
                if n >= 2:
                    pe.wait_ge(o_stored, heads + (n - 1))
                for t in range(2):
                    ins = pe.matmul(ps_m[STACK:STACK + PARTS, t * P:(t + 1) * P], neg_parts[:, n % 2, t, 0:PARTS],
                                    ident_bf[:], start=True, stop=True)
                ins.then_inc(rows_ps, 1)

            def scores(base, heads, g):
                n, u = g // UNITS, g % UNITS
                slot = n % SLOTS
                if u == 0:
                    pe.wait_ge(rows_ready, heads + n + 1)
                    if slot >= 2:
                        pe.wait_ge(ones_set, 2)
                if g >= 2:
                    pe.wait_ge(exp_done, base + (g - 1))
                if u in PE_UNITS:
                    bias = mask_turned[:, PE_UNITS.index(u)].rearrange("p k q -> p (k q)")
                    for c in range(2):
                        pe.matmul(ps_b[:, g % 2, c * 512:(c + 1) * 512], ident_bf[:],
                                  bias[:, c * 512:(c + 1) * 512], start=True, stop=False, skip_group_check=True)
                for k in range(UT):
                    key = u * UK + k * P
                    ins = pe.matmul(ps_b[:, g % 2, k * Q:(k + 1) * Q], kst[slot][0:ROWS, key:key + P],
                                    qst[0:ROWS, slot, :], start=u not in PE_UNITS, stop=True,
                                    skip_group_check=u in PE_UNITS)
                ins.then_inc(b_ps, 1)

            def values(base, heads, g):
                n, u = g // UNITS, g % UNITS
                if masks(g) == "pool":
                    pe.wait_ge(pool_masked, heads * len(POOL_UNITS) + masked("pool", g))
                elif masks(g) == "dve":
                    pe.wait_ge(dve_masked, heads * 2 * len(DVE_UNITS) + 2 * masked("dve", g))
                else:
                    pe.wait_ge(exp_done, base + (g + 1))
                if u == 0:
                    pe.wait_ge(vh_ready, heads + n + 1)
                    if n >= 1:
                        pe.wait_ge(oT_ready, heads + n)
                for k in range(UT):
                    ins = pe.matmul(ps_v[32 * k:32 * k + 32, 0:Q], Vh[:, n % 2, u * UT + k, :],
                                    probs[:, g % 4, k * Q:(k + 1) * Q], start=(u == 0), stop=(u == UNITS - 1))
                ins.then_inc(pv_done, 1)

            def fold_o(heads, n):
                pe.wait_ge(oT_ready, heads + n + 1)
                for t in range(2):
                    ins = pe.matmul(o_cols[:, t, 0:D + 1], oT[:, n % 2, t * P:(t + 1) * P], fold[:, 0:D + 1],
                                    start=True, stop=True)
                ins.then_inc(o_ps, 1)

            pe.wait_ge(k_rest, 2 * B * NC + 1)
            for j in range(2):
                pe.wait_ge(v_stored[j], B * NC + 1)
            pe.wait_ge(masks_ready, 4 * NC)
            pe.wait_ge(consts, 3)
            pe.wait_ge(ones_set, 1)
            def turn_attn(first, last):
                for t in range(first, last):
                    pe.wait_ge(attn_ready, t + 1)
                    for a in range(KIN):
                        ins = pe.transpose(BANK[t][:, a * P:(a + 1) * P], attn[:, t, a * P:(a + 1) * P], ident[:])
                    ins.then_inc(aT_ps, 1)

            def project_attn(first, last):
                pe.wait_ge(wo_in, 16)
                for t in range(first, last):
                    pe.wait_ge(aT_ready, t + 1)
                    for a in range(KIN):
                        ins = pe.matmul(projected(t), aT[:, t, a * P:(a + 1) * P], w_o[:, a, :],
                                        start=(a == 0), stop=(a == KIN - 1))
                    ins.then_inc(wo_ps, 1)

            for a in range(LEAD_A):
                for t in range(2):
                    scores_for_max(0, a, t)
                if a == UNITS + 2:
                    turn_max(0, 0)
                if a >= LEAD_A - LEAD_B:
                    scores(0, 0, a - (LEAD_A - LEAD_B))

            def step(base, heads, s):
                n = s // UNITS
                if s + LEAD_A < STEPS:
                    scores_for_max(base, s + LEAD_A, 0)
                if s % UNITS == 1 and s >= UNITS:
                    fold_o(heads, n - 1)
                if s + LEAD_B < STEPS:
                    scores(base, heads, s + LEAD_B)
                if s % UNITS == 4 and n + 1 < NH:
                    turn_max(heads, n + 1)
                if s + LEAD_A < STEPS:
                    scores_for_max(base, s + LEAD_A, 1)
                values(base, heads, s)

            for s in range(FIRST):
                step(0, 0, s)
            body = SLOTS * UNITS
            with pe.Fori(0, (LAST - FIRST) // body) as i:
                for s in range(FIRST, FIRST + body):
                    step(i * body, i * SLOTS, s)
            for s in range(LAST, STEPS):
                step(0, 0, s)
            pe.wait_ge(a_max, 2 * STEPS)
            turn_attn(0, T // 2)
            pe.wait_ge(o_stored, NH - 1)
            fold_o(0, NH - 1)

            project_attn(0, T // 2)
            turn_attn(T // 2, T)
            project_attn(T // 2, T)
            transpose_xn(1, 0)
            pe.wait_ge(self_in, 48)
            pe.wait_ge(xnT_ready, 2 * T)
            for m, w in enumerate((self_w[:, 0], self_w[:, 1])):
                for e in range(KIN):
                    for a in range(KIN):
                        ins = pe.matmul(BANK[4 + 2 * m + e], w[:, a, e * P:(e + 1) * P], xnT[:, a, :],
                                        start=(a == 0), stop=(a == KIN - 1))
                    ins.then_inc(qk2_ps, 1)
            pe.wait_ge(small_in, 64)

            def self_values(tiles):
                for t in tiles:
                    for a in range(KIN):
                        pe.matmul(BANK[t][:, 0:E], xnT[:, a, t * P:(t + 1) * P], self_w[:, 2, a, :],
                                  start=(a == 0), stop=False)
                    pe.matmul(BANK[t][:, 0:E], ones_row[:], bias_v[:], start=False, stop=True).then_inc(v2_ps, 1)

            self_values(range(T // 2))
            pe.wait_ge(qk2_ready, 2 * KIN)
            for t in range(T):
                for e in range(KIN):
                    ins = pe.matmul(BANK[4 + t][:, 0:P], q2T[:, e, t * P:(t + 1) * P], k2T[:, e, t * P:(t + 1) * P],
                                    start=(e == 0), stop=(e == KIN - 1))
                ins.then_inc(s2_ps, 1)
            self_values(range(T // 2, T))
            for t in range(T):
                pe.wait_ge(p2_ready, t + 1)
                pe.wait_ge(v2_ready, t + 1)
                pe.transpose(BANK[t][:, 256:384], p2[:, t, :], ident[:]).then_inc(p2T_ps, 1)
            for t in range(T):
                pe.wait_ge(p2T_ready, t + 1)
                pe.matmul(BANK[4 + t][:, 256:512], p2T[:, t, :], v2[:, t, :], start=True, stop=True).then_inc(o2_ps, 1)
            transpose_xn(2, 4)
            pe.wait_ge(xnT_ready, 3 * T)
            for t in range(T):
                for a in range(KIN):
                    ins = pe.matmul(ps_m[:, t * NE:(t + 1) * NE], xnT[:, a, t * P:(t + 1) * P], w_g[:, a, :],
                                    start=(a == 0), stop=(a == KIN - 1))
            ins.then_inc(gate_ps, 1)

            def up(base, e):
                pe.wait_ge(up_split, base + (e + 1))
                for f in range(FT):
                    if e or f >= 2:
                        pe.wait_ge(hid_ready, base * FT + (FT * e + f - 1))
                    for m in range(2):
                        for a in range(KIN):
                            col = m * F + f * P
                            ins = product(BANK[2 * (f % 2) + m], up_high[:, e % 2, a, col:col + P],
                                          up_low[:, e % 2, a, col:col + P], xnT_high[:, a, :], xnT_low[:, a, :],
                                          a == 0, a == KIN - 1)
                    ins.then_inc(up_ps, 1)

            def down(base, e):
                pe.wait_ge(hid_split, base * FT + FT * (e + 1))
                pe.wait_ge(down_split, base + (e + 1))
                pe.wait_ge(summed, base * T + (T * e + 1))
                for t in range(T):
                    for f in range(FT):
                        cols = slice(t * P, (t + 1) * P)
                        ins = product(BANK[4 + t][:, 0:E], hid_high[:, e % 2, f, cols], hid_low[:, e % 2, f, cols],
                                      down_high[:, e % 2, f, :], down_low[:, e % 2, f, :], f == 0, f == FT - 1)
                    ins.then_inc(down_ps, 1)

            pe.wait_ge(xnT_split, T)
            up(0, 0)
            pe.wait_ge(gate_sub, 1)
            with pe.Fori(0, NE // 2 - 1) as i:
                for j in range(2):
                    up(i * 2, j + 1)
                    down(i * 2, j)
            up(0, NE - 1)
            down(0, NE - 2)
            down(0, NE - 1)


def kernel(x, ctx_1024, mask_1x1xSxS2_bk0, L0_xattn_wq, L0_xattn_wk, L0_xattn_wv, L0_xattn_wo, L0_attn_Wq,
           L0_attn_bq, L0_attn_Wk, L0_attn_bk, L0_attn_Wv, L0_attn_bv, L0_ffn_gate_w, L0_ffn_gate_up_w,
           L0_ffn_down_w):
    import numpy as np
    import concourse.bacc as bacc
    from concourse.bass_utils import run_bass_kernel_spmd

    def turned(w):
        return np.asarray(w).T.reshape(KIN, P, E).transpose(1, 0, 2)

    mask = np.asarray(mask_1x1xSxS2_bk0).reshape(Q, S)
    units = mask.T.reshape(UNITS, UK, Q)
    turned_mask = np.concatenate([units[u] for u in PE_UNITS + DVE_UNITS + POOL_UNITS])
    turned_mask = turned_mask.reshape(KT, P, Q).transpose(1, 0, 2)
    chunks = np.asarray(ctx_1024).reshape(B * NC, CK, KIN, P).transpose(0, 3, 2, 1)
    ups = np.asarray(L0_ffn_gate_up_w).reshape(NE, KIN, P, 2 * F).transpose(0, 2, 1, 3)
    arrays = {
        "x": np.asarray(x).reshape(B * Q, E), "ctx_in": chunks, "mask_q": mask, "mask_k": turned_mask,
        "wq": turned(L0_xattn_wq), "wk": turned(L0_xattn_wk), "wv": turned(L0_xattn_wv), "wo": turned(L0_xattn_wo),
        "sq": turned(L0_attn_Wq), "bq": np.asarray(L0_attn_bq).reshape(KIN, P).T,
        "sk": turned(L0_attn_Wk), "bk": np.asarray(L0_attn_bk).reshape(KIN, P).T,
        "sv": turned(L0_attn_Wv), "bv": L0_attn_bv,
        "gate_w": L0_ffn_gate_w, "up_w": ups, "down_w": L0_ffn_down_w,
    }
    arrays = {name: np.ascontiguousarray(a) for name, a in arrays.items()}
    nc = bacc.Bacc("TRN2", target_bir_lowering=False, num_devices=1)
    args = {name: nc.dram_tensor(name, a.shape, mybir.dt.from_np(a.dtype), kind="ExternalInput").ap()
            for name, a in arrays.items()}
    out = nc.dram_tensor("out", (B * Q, E), F32, kind="ExternalOutput").ap()
    perceiver_block(nc, out=out, **args)
    got = run_bass_kernel_spmd(nc, [arrays], core_ids=[0])
    return got.results[0]["out"].reshape(B, Q, E)
```
